# Optimizing a Trainium2 kernel written in Bass

```python
import numpy as np
import jax
import jax.numpy as jnp

def _softmax(x, axis=-1):
    return jax.nn.softmax(x, axis=axis)

def _gelu(x):
    return jax.nn.gelu(x, approximate=True)

def _silu(x):
    return jax.nn.silu(x)

def _sigmoid(x):
    return jax.nn.sigmoid(x)

def _layernorm(x, axis=-1, eps=1e-05):
    m = jnp.mean(x, axis=axis, keepdims=True)
    v = jnp.var(x, axis=axis, keepdims=True)
    return (x - m) / jnp.sqrt(v + eps)

def _scatter_add(tgt, idx, src, axis=0):
    return tgt.at[idx].add(src)

def _segment_sum(src, seg, n):
    return jax.ops.segment_sum(src, seg, n)
kernel_name = 'mk_seq_postln_d1_jaxref_r4_73cf97'

def setup_inputs(seed: int=0):
    np.random.seed(seed)
    _w = jnp.asarray

    def _L0_attn_setup():
        import jax, jax.numpy as jnp
        import numpy as np
        HIDDEN = 512
        NUM_HEADS = 16
        HEAD_DIM = 128
        BLOCK_SIZE = 64
        NUM_ACTIVE_BLOCKS = 4
        NEG_INF = -1e+30

        def _block_diagonal_additive_mask(seq_len: int) -> jnp.ndarray:
            bandwidth = NUM_ACTIVE_BLOCKS // 2
            bid = jnp.arange(seq_len) // BLOCK_SIZE
            active = jnp.abs(bid[:, None] - bid[None, :]) <= bandwidth
            return jnp.where(active, 0.0, NEG_INF).astype(jnp.float32)
        key = jax.random.key(seed)
        k0, k1, k2, k3, k4 = jax.random.split(key, 5)
        B, S = (2, 512)
        scale = 1.0 / np.sqrt(HIDDEN)
        return {'hidden_states': jax.random.normal(k0, (B, S, HIDDEN), dtype=jnp.float32), 'Wq': jax.random.normal(k1, (HIDDEN, NUM_HEADS * HEAD_DIM), dtype=jnp.float32) * scale, 'Wk': jax.random.normal(k2, (HIDDEN, NUM_HEADS * HEAD_DIM), dtype=jnp.float32) * scale, 'Wv': jax.random.normal(k3, (HIDDEN, NUM_HEADS * HEAD_DIM), dtype=jnp.float32) * scale, 'Wo': jax.random.normal(k4, (NUM_HEADS * HEAD_DIM, HIDDEN), dtype=jnp.float32) * scale}
    _L0_attn_in = _L0_attn_setup()

    def _L0_ffn_setup():
        import jax, jax.numpy as jnp
        import numpy as np
        CAPACITY = 0.125
        HEAD_DIM = 128
        N_HEADS = 16
        N_KV_HEADS = 8
        ROPE_THETA = 10000.0
        EPS = 1e-06

        def _rms_norm(x, w):
            return x * jax.lax.rsqrt(jnp.mean(x * x, axis=-1, keepdims=True) + EPS) * w

        def _rotate_half(t):
            h = t.shape[-1] // 2
            return jnp.concatenate([-t[..., h:], t[..., :h]], axis=-1)
        key = jax.random.key(seed)
        ks = jax.random.split(key, 12)
        B, T, D = (4, 1024, 512)
        I = 2048
        s = 0.02
        return {'hidden_states': jax.random.normal(ks[0], (B, T, D), jnp.float32), 'w_router': jax.random.normal(ks[1], (D,), jnp.float32) * s, 'wq': jax.random.normal(ks[2], (D, N_HEADS * HEAD_DIM), jnp.float32) * s, 'bq': jnp.zeros((N_HEADS * HEAD_DIM,), jnp.float32), 'wk': jax.random.normal(ks[3], (D, N_KV_HEADS * HEAD_DIM), jnp.float32) * s, 'bk': jnp.zeros((N_KV_HEADS * HEAD_DIM,), jnp.float32), 'wv': jax.random.normal(ks[4], (D, N_KV_HEADS * HEAD_DIM), jnp.float32) * s, 'bv': jnp.zeros((N_KV_HEADS * HEAD_DIM,), jnp.float32), 'wo': jax.random.normal(ks[5], (N_HEADS * HEAD_DIM, D), jnp.float32) * s, 'w_gate': jax.random.normal(ks[6], (D, I), jnp.float32) * s, 'w_up': jax.random.normal(ks[7], (D, I), jnp.float32) * s, 'w_down': jax.random.normal(ks[8], (I, D), jnp.float32) * s, 'ln1_w': jnp.ones((D,), jnp.float32), 'ln2_w': jnp.ones((D,), jnp.float32)}
    _L0_ffn_in = _L0_ffn_setup()
    _d = {'L0_attn_hidden_states': _L0_attn_in['hidden_states'], 'L0_attn_Wq': _L0_attn_in['Wq'], 'L0_attn_Wk': _L0_attn_in['Wk'], 'L0_attn_Wv': _L0_attn_in['Wv'], 'L0_attn_Wo': _L0_attn_in['Wo'], 'L0_ffn_w_router': _L0_ffn_in['w_router'], 'L0_ffn_wq': _L0_ffn_in['wq'], 'L0_ffn_bq': _L0_ffn_in['bq'], 'L0_ffn_wk': _L0_ffn_in['wk'], 'L0_ffn_bk': _L0_ffn_in['bk'], 'L0_ffn_wv': _L0_ffn_in['wv'], 'L0_ffn_bv': _L0_ffn_in['bv'], 'L0_ffn_wo': _L0_ffn_in['wo'], 'L0_ffn_w_gate': _L0_ffn_in['w_gate'], 'L0_ffn_w_up': _L0_ffn_in['w_up'], 'L0_ffn_w_down': _L0_ffn_in['w_down'], 'L0_ffn_ln1_w': _L0_ffn_in['ln1_w'], 'L0_ffn_ln2_w': _L0_ffn_in['ln2_w']}
    _x0 = _d['L0_attn_hidden_states']
    _d['L0_attn_hidden_states'] = jax.random.normal(jax.random.fold_in(jax.random.key(seed), 1), (2, 1024, 512), dtype=_x0.dtype)
    del _x0
    return _d

def reference(L0_attn_hidden_states, L0_attn_Wq, L0_attn_Wk, L0_attn_Wv, L0_attn_Wo, L0_ffn_w_router, L0_ffn_wq, L0_ffn_bq, L0_ffn_wk, L0_ffn_bk, L0_ffn_wv, L0_ffn_bv, L0_ffn_wo, L0_ffn_w_gate, L0_ffn_w_up, L0_ffn_w_down, L0_ffn_ln1_w, L0_ffn_ln2_w):

    def _L0_attn_ref(hidden_states, Wq, Wk, Wv, Wo):
        import jax, jax.numpy as jnp
        import numpy as np
        HIDDEN = 512
        NUM_HEADS = 16
        HEAD_DIM = 128
        BLOCK_SIZE = 64
        NUM_ACTIVE_BLOCKS = 4
        NEG_INF = -1e+30

        def _block_diagonal_additive_mask(seq_len: int) -> jnp.ndarray:
            bandwidth = NUM_ACTIVE_BLOCKS // 2
            bid = jnp.arange(seq_len) // BLOCK_SIZE
            active = jnp.abs(bid[:, None] - bid[None, :]) <= bandwidth
            return jnp.where(active, 0.0, NEG_INF).astype(jnp.float32)
        B, S, _ = hidden_states.shape
        scaling = HEAD_DIM ** (-0.5)

        def split_heads(x):
            return x.reshape(B, S, NUM_HEADS, HEAD_DIM).transpose(0, 2, 1, 3)
        q = split_heads(hidden_states @ Wq)
        k = split_heads(hidden_states @ Wk)
        v = split_heads(hidden_states @ Wv)
        mask = _block_diagonal_additive_mask(S)
        scores = jnp.einsum('bhsd,bhtd->bhst', q, k) * scaling + mask[None, None]
        attn = jax.nn.softmax(scores.astype(jnp.float32), axis=-1).astype(q.dtype)
        out = jnp.einsum('bhst,bhtd->bhsd', attn, v)
        out = out.transpose(0, 2, 1, 3).reshape(B, S, NUM_HEADS * HEAD_DIM)
        return out @ Wo

    def _L0_ffn_ref(hidden_states, w_router, wq, bq, wk, bk, wv, bv, wo, w_gate, w_up, w_down, ln1_w, ln2_w):
        import jax, jax.numpy as jnp
        import numpy as np
        CAPACITY = 0.125
        HEAD_DIM = 128
        N_HEADS = 16
        N_KV_HEADS = 8
        ROPE_THETA = 10000.0
        EPS = 1e-06

        def _rms_norm(x, w):
            return x * jax.lax.rsqrt(jnp.mean(x * x, axis=-1, keepdims=True) + EPS) * w

        def _rotate_half(t):
            h = t.shape[-1] // 2
            return jnp.concatenate([-t[..., h:], t[..., :h]], axis=-1)
        B, T, D = hidden_states.shape
        k = max(1, int(T * CAPACITY))
        scores = jnp.einsum('btd,d->bt', hidden_states, w_router)
        _, idx = jax.lax.top_k(scores, k)
        idx = jnp.sort(idx, axis=-1)
        b = jnp.arange(B)[:, None]
        sel = hidden_states[b, idx]
        sel_scores = scores[b, idx]
        S = B * k
        x = sel.reshape(S, D)
        pos = idx.reshape(S)
        inv_freq = 1.0 / ROPE_THETA ** (jnp.arange(0, HEAD_DIM, 2, dtype=jnp.float32) / HEAD_DIM)
        ang = pos.astype(jnp.float32)[:, None] * inv_freq
        cos = jnp.concatenate([jnp.cos(ang), jnp.cos(ang)], axis=-1)[:, None, :]
        sin = jnp.concatenate([jnp.sin(ang), jnp.sin(ang)], axis=-1)[:, None, :]
        h = _rms_norm(x, ln1_w)
        q = (h @ wq + bq).reshape(S, N_HEADS, HEAD_DIM)
        kk = (h @ wk + bk).reshape(S, N_KV_HEADS, HEAD_DIM)
        v = (h @ wv + bv).reshape(S, N_KV_HEADS, HEAD_DIM)
        q = q * cos + _rotate_half(q) * sin
        kk = kk * cos + _rotate_half(kk) * sin
        rep = N_HEADS // N_KV_HEADS
        kk = jnp.repeat(kk, rep, axis=1)
        v = jnp.repeat(v, rep, axis=1)
        att = jnp.einsum('shd,thd->hst', q, kk) / np.sqrt(HEAD_DIM)
        causal = jnp.tril(jnp.ones((S, S), bool))
        att = jnp.where(causal[None], att, jnp.finfo(att.dtype).min)
        att = jax.nn.softmax(att, axis=-1)
        attn_out = jnp.einsum('hst,thd->shd', att, v).reshape(S, N_HEADS * HEAD_DIM) @ wo
        x1 = x + attn_out
        h2 = _rms_norm(x1, ln2_w)
        mlp = jax.nn.silu(h2 @ w_gate) * (h2 @ w_up) @ w_down
        processed = x1 + mlp
        gate = jax.nn.sigmoid(sel_scores).reshape(S, 1)
        gated = gate * processed + (1.0 - gate) * x
        output = hidden_states.at[b, idx].set(gated.reshape(B, k, D))
        return output
    x = L0_attn_hidden_states
    x = _layernorm(x + _L0_attn_ref(x, L0_attn_Wq, L0_attn_Wk, L0_attn_Wv, L0_attn_Wo), axis=-1)
    x = _layernorm(x + _L0_ffn_ref(x, L0_ffn_w_router, L0_ffn_wq, L0_ffn_bq, L0_ffn_wk, L0_ffn_bk, L0_ffn_wv, L0_ffn_bv, L0_ffn_wo, L0_ffn_w_gate, L0_ffn_w_up, L0_ffn_w_down, L0_ffn_ln1_w, L0_ffn_ln2_w), axis=-1)
    return x

_drawn_inputs = setup_inputs


def setup_inputs(seed=0):
    import zlib

    import numpy as np

    out = dict(_drawn_inputs(seed))
    spreads = {'L0_ffn_bq': (0.0, 0.8),
     'L0_ffn_bk': (0.0, 0.8),
     'L0_ffn_bv': (0.0, 0.679),
     'L0_ffn_ln1_w': (1.0, 0.6),
     'L0_ffn_ln2_w': (1.0, 0.6)}
    factors = {'L0_ffn_w_router': 2.962,
     'L0_ffn_wq': 8.0,
     'L0_ffn_wk': 8.0,
     'L0_ffn_wv': 5.487,
     'L0_ffn_wo': 3.76,
     'L0_ffn_w_gate': 4.507,
     'L0_ffn_w_up': 4.394,
     'L0_ffn_w_down': 4.432}
    for name, (base, spread) in spreads.items():
        noise = np.random.default_rng([zlib.crc32(name.encode()), seed]).standard_normal(out[name].shape)
        drawn = base * np.exp(spread * noise) if base else spread * noise
        out[name] = jnp.asarray(drawn.astype(out[name].dtype))
    for name, factor in factors.items():
        out[name] = (out[name] * factor).astype(out[name].dtype)
    return out
```

```python
from contextlib import ExitStack

import numpy as np

import concourse.bass as bass
from concourse import mybir

F32 = mybir.dt.float32
F32R = mybir.dt.float32r
BF16 = mybir.dt.bfloat16
I32 = mybir.dt.int32
ALU = mybir.AluOpType
ACT = mybir.ActivationFunctionType
AX = mybir.AxisListType.X

P = 128
NB, T, D = 2, 1024, 512
KT = D // P
TT = T // P
HD = 128
NH = 16
BLK = 64
HG = 2
NG = NH // HG
GW = HG * HD
PIECE = KT * GW
SCALE = float(HD) ** -0.5
NEG = -1e30
LN_EPS, RMS_EPS = 1e-5, 1e-6
KSEL = T // 8
NKV = 8
FF = 2048
NSEL = NB * KSEL
SPLIT_SLOTS, RAW_SLOTS = 5, 2
O_SLOTS = 3


class Signal:

    def __init__(self, sem):
        self.sem, self.count = sem, 0


class Queue:

    def __init__(self):
        self.items, self.reached = [], {}

    def wait(self, *tokens):
        for token in tokens:
            if token is None:
                continue
            sig, value = token
            if self.reached.get(sig, 0) < value:
                self.reached[sig] = value
                self.items.append(("wait", sig.sem, value))

    def do(self, fn, signal=None, by=1):
        if signal is None:
            self.items.append(("run", fn, None, 0))
            return None
        signal.count += by
        self.items.append(("run", fn, signal.sem, by))
        return signal, signal.count

    def replay(self, eng):
        for item in self.items:
            if item[0] == "wait":
                eng.wait_ge(item[1], item[2])
            else:
                ins = item[1](eng)
                if item[2] is not None:
                    ins.then_inc(item[2], item[3])


def strided(ap, offset, step, count, width):
    return bass.AP(tensor=ap.tensor, offset=ap.offset + offset,
                   ap=[list(ap.ap[0]), [step, count], [1, width]])


def build(nc, x, Wq, Wk, Wv, Wo, w_router, wq, bq, wk, bk, wv, bv, wo, w_gate, w_up, w_down,
          ln1_w, ln2_w, rope, out):
    with ExitStack() as ctx:
        def sb(name, shape, dt=F32):
            return ctx.enter_context(nc.sbuf_tensor(name, shape, dt))

        def bank(name):
            return ctx.enter_context(nc.psum_tensor(name, [P, 512], F32))

        def signal(name):
            return Signal(ctx.enter_context(nc.semaphore(name)))

        y_dram = [nc.dram_tensor(f"y_dram{b}", [T, D], F32, kind="Internal").ap() for b in range(NB)]

        NHEADS = NB * NH

        XT_N, QK_N, V_N, PT_N, O_N = KT * T, T, TT * GW, TT * 3 * P, T
        sizes = dict(xT=2 * XT_N, q=2 * QK_N, k=2 * QK_N, v=2 * V_N, pT=2 * PT_N, oT=2 * O_SLOTS * O_N,
                     w=2 * SPLIT_SLOTS * PIECE)
        start, at = {}, 0
        for name, n in sizes.items():
            start[name] = at
            at += n
        arena = sb("arena", [P, at], F32R)

        def carve(offset, *shape):
            n = int(np.prod(shape))
            view = arena[:, offset:offset + n]
            if len(shape) == 2:
                return view.rearrange("p (a b) -> p a b", a=shape[0])
            if len(shape) == 3:
                return view.rearrange("p (a b c) -> p a b c", a=shape[0], b=shape[1])
            return view

        xT = [carve(start["xT"] + i * XT_N, KT, T) for i in range(2)]
        qT = [carve(start["q"] + i * QK_N, T) for i in range(2)]
        kT = [carve(start["k"] + i * QK_N, T) for i in range(2)]
        vv = [carve(start["v"] + i * V_N, TT, GW) for i in range(2)]
        pT = [carve(start["pT"] + i * PT_N, TT * 3 * P) for i in range(2)]
        oT = [[carve(start["oT"] + (2 * s + i) * O_N, T) for i in range(2)] for s in range(O_SLOTS)]
        wsp = [[carve(start["w"] + (2 * s + i) * PIECE, PIECE) for i in range(2)] for s in range(SPLIT_SLOTS)]
        yacc = sb("yacc", [P, TT, D])
        wraw = [sb(f"wraw{i}", [P, PIECE]) for i in range(RAW_SLOTS)]
        prob = [sb(f"prob{i}", [P, 3 * P]) for i in range(2)]
        work = [sb(f"work{i}", [P, D]) for i in range(6)]
        ident = sb("ident", [P, P])
        mask_l = sb("mask_l", [P, P], BF16)
        mask_r = sb("mask_r", [P, P], BF16)
        stat = sb("stat", [P, 64])
        router = sb("router", [P, D])

        proj = [bank("proj0"), bank("proj1")]
        sbank = [bank("s0"), bank("s1")]
        tbank = bank("tp")
        obank = [bank("o0"), bank("o1")]
        ybank = bank("y")

        pe, dve, act, pool, sp = Queue(), Queue(), Queue(), Queue(), Queue()

        const_ready = signal("const_ready")
        raw_loaded = [signal(f"raw_loaded{i}") for i in range(RAW_SLOTS)]
        w_hi_done, w_lo_done, w_used = signal("w_hi_done"), signal("w_lo_done"), signal("w_used")
        x_loaded = [signal(f"x_loaded{i}") for i in range(2)]
        x_turned, x_hi_done, x_lo_done = signal("x_turned"), signal("x_hi_done"), signal("x_lo_done")
        projected, proj_hi_done, proj_lo_done = (signal("projected"), signal("proj_hi_done"),
                                                 signal("proj_lo_done"))
        scored, max_done, negmax_done, exp_done, recip_done, norm_done = (
            signal("scored"), signal("max_done"), signal("negmax_done"), signal("exp_done"),
            signal("recip_done"), signal("norm_done"))
        turned, pt_hi_done, pt_lo_done = signal("turned"), signal("pt_hi_done"), signal("pt_lo_done")
        attended, o_hi_done, o_lo_done = signal("attended"), signal("o_hi_done"), signal("o_lo_done")
        y_made, y_added = signal("y_made"), signal("y_added")
        resid_loaded = [signal(f"resid_loaded{t}") for t in range(TT)]

        masks_ready = signal("masks_ready")
        t = pool.do(lambda e: e.memset(ident[:], 0.0), const_ready)
        pool.wait(t)
        consts = pool.do(lambda e: e.affine_select(out=ident[:], in_=ident[:], compare_op=ALU.not_equal, fill=1.0,
                                                   base=0, pattern=[[-1, P]], channel_multiplier=1), const_ready)
        dve.do(lambda e: e.memset(mask_l[:], 0.0), masks_ready)
        t = dve.do(lambda e: e.memset(mask_r[:], 0.0), masks_ready)
        dve.wait(t)
        dve.do(lambda e: e.memset(mask_l[0:1, 0:BLK], 1.0), masks_ready)
        dve.do(lambda e: e.memset(mask_l[32:33, BLK:P], 1.0), masks_ready)
        dve.do(lambda e: e.memset(mask_r[32:33, 0:BLK], NEG), masks_ready)
        t = dve.do(lambda e: e.memset(mask_r[0:1, BLK:P], NEG), masks_ready)
        pe.wait(consts, t)

        def three_passes(out_ap, pairs, start, stop, tail_signal=None, skip=False):
            tok = None
            n = len(pairs)
            for i, (l, r) in enumerate(pairs):
                for j, (a, b) in enumerate(((0, 0), (0, 1), (1, 0))):
                    last = i == n - 1 and j == 2
                    tok = pe.do(lambda e, a=l[a], b=r[b], s=start and i == 0 and j == 0, f=stop and last:
                                e.matmul(out_ap, a, b, start=s, stop=f, skip_group_check=skip),
                                tail_signal if last else None)
            return tok

        def split_from_psum(src, hi, lo, ready, hi_sig, lo_sig, *free):
            act.wait(ready, *free)
            t_hi = act.do(lambda e: e.activation(hi, src, ACT.Copy), hi_sig)
            dve.wait(ready, t_hi, *free)
            t_lo = dve.do(lambda e: e.tensor_tensor(lo, src, hi.bitcast(F32), ALU.subtract), lo_sig)
            return t_hi, t_lo

        stream = []

        def columns(w, c):
            return w[:, c * GW:(c + 1) * GW].rearrange("(k p) n -> p k n", p=P)

        def rows(w, c):
            return w[c * GW:(c + 1) * GW, :].rearrange("(k p) n -> p k n", p=P)

        for b in range(NB):
            for g in range(NG):
                stream += [(("q", b, g), columns(Wq, g)), (("k", b, g), columns(Wk, g)),
                           (("v", b, g), columns(Wv, g))]
                G = b * NG + g
                if G >= 1:
                    stream.append((("o", *divmod(G - 1, NG)), rows(Wo, (G - 1) % NG)))
        stream.append((("o", NB - 1, NG - 1), rows(Wo, NG - 1)))
        for b in range(NB):
            stream += [(("q2", b, c), columns(wq, c)) for c in range(NH * HD // GW)]
            stream += [(("k2", b, c), columns(wk, c)) for c in range(NKV * HD // GW)]
            stream += [(("v2", b, c), columns(wv, c)) for c in range(NKV * HD // GW)]
        stream += [(("o2", 0, c), rows(wo, c)) for c in range(NH * HD // GW)]
        for c in range(FF // GW):
            stream += [(("g2", 0, c), columns(w_gate, c)), (("u2", 0, c), columns(w_up, c))]
            if c >= 1:
                stream.append((("d2", 0, c - 1), rows(w_down, c - 1)))
        stream.append((("d2", 0, FF // GW - 1), rows(w_down, FF // GW - 1)))
        number = {key: n for n, (key, _) in enumerate(stream)}
        split_tokens, slot_of, raw_free = {}, {}, {}
        free_slots = [(s, None) for s in range(SPLIT_SLOTS)]
        issued = [0]

        def pump():
            while issued[0] < len(stream) and free_slots:
                n = issued[0]
                slot, used = free_slots.pop(0)
                key, src = stream[n]
                slot_of[n] = slot
                raw, (hi, lo) = wraw[n % RAW_SLOTS], wsp[slot]
                sp.wait(*raw_free.get(n - RAW_SLOTS, ()))
                dst = raw[:].rearrange("p (k n) -> p k n", k=src.shape[1])
                loaded = sp.do(lambda e, dst=dst, src=src: e.dma_start(dst, src), raw_loaded[n % RAW_SLOTS], 16)
                pool.wait(loaded, used)
                t_hi = pool.do(lambda e, hi=hi, raw=raw: e.tensor_copy(hi, raw[:]), w_hi_done)
                pool.wait(t_hi)
                t_lo = pool.do(lambda e, hi=hi, lo=lo, raw=raw:
                               e.tensor_tensor(lo, raw[:], hi.bitcast(F32), ALU.subtract), w_lo_done)
                split_tokens[n] = (t_hi, t_lo)
                raw_free[n] = (t_lo,)
                issued[0] += 1

        def piece(key):
            n = number[key]
            pe.wait(*split_tokens[n])
            return wsp[slot_of[n]]

        def retire(key, token):
            free_slots.append((slot_of[number[key]], token))
            pump()

        proj_free = [(), ()]
        proj_turn = [0]

        def take_proj():
            i = proj_turn[0] % 2
            proj_turn[0] += 1
            pe.wait(*proj_free[i])
            return i

        work_free = [None] * 6
        xT_ready = {}
        xT_last_use = {}

        def load_x(b, t):
            slot = t % 2
            sp.wait(work_free[slot])
            return sp.do(lambda e: e.dma_start(work[slot][:], x[b, t * P:(t + 1) * P, :]), x_loaded[slot], 16)

        def turn_x(b, t):
            slot = t % 2
            loaded = load_x(b, t)
            i = take_proj()
            pe.wait(loaded)
            for k in range(KT):
                tok = pe.do(lambda e, k=k: e.transpose(proj[i][:, k * P:(k + 1) * P],
                                                       work[slot][:, k * P:(k + 1) * P], ident[:]),
                            x_turned if k == KT - 1 else None)
            work_free[slot] = tok
            src = proj[i][:, :].rearrange("p (k n) -> p k n", k=KT)
            cols = slice(t * P, (t + 1) * P)
            xT_ready[t] = split_from_psum(src, xT[0][:, :, cols], xT[1][:, :, cols], tok,
                                          x_hi_done, x_lo_done, xT_last_use.get(t))
            proj_free[i] = xT_ready[t]

        def load_resid(b, t, free=None):
            sp.wait(free)
            return sp.do(lambda e: e.dma_start(yacc[:, t, :], x[b, t * P:(t + 1) * P, :]), resid_loaded[t], 16)

        CH = 512
        q_ready, k_ready, v_ready = {}, {}, {}
        s_done = {}
        pv_done = {}

        def project_qk(H, which, c):
            b, h = divmod(H, NH)
            w = piece((which, b, h // HG))
            for t in range(c * 4, c * 4 + 4):
                pe.wait(*xT_ready[t])
            i = take_proj()
            hcols = slice((h % HG) * HD, (h % HG + 1) * HD)
            w4 = [half.rearrange("p (k n) -> p k n", k=KT) for half in w]
            cols = slice(c * CH, (c + 1) * CH)
            tok = three_passes(proj[i][:, :], [([w4[0][:, k, hcols], w4[1][:, k, hcols]],
                                                [xT[0][:, k, cols], xT[1][:, k, cols]]) for k in range(KT)],
                               True, True, projected)
            for t in range(c * 4, c * 4 + 4):
                xT_last_use[t] = tok
            dst = qT if which == "q" else kT
            last_reader = s_done.get((H - 1, {("q", 0): 3, ("q", 1): 7, ("k", 0): 4, ("k", 1): 7}[which, c]))
            ready = split_from_psum(proj[i][:, :], dst[0][:, cols], dst[1][:, cols], tok,
                                    proj_hi_done, proj_lo_done, last_reader)
            proj_free[i] = ready
            (q_ready if which == "q" else k_ready)[H, c] = ready
            if h % HG == HG - 1 and c == 1:
                retire((which, b, h // HG), tok)

        def project_v(G, t):
            b, g = divmod(G, NG)
            w = piece(("v", b, g))
            pe.wait(*xT_ready[t])
            i = take_proj()
            w4 = [half.rearrange("p (k n) -> p k n", k=KT) for half in w]
            cols = slice(t * P, (t + 1) * P)
            tok = three_passes(proj[i][:, 0:GW], [([xT[0][:, k, cols], xT[1][:, k, cols]],
                                                   [w4[0][:, k, :], w4[1][:, k, :]]) for k in range(KT)],
                               True, True, projected)
            xT_last_use[t] = tok
            last_reader = pv_done.get((HG * G - 1, t))
            ready = split_from_psum(proj[i][:, 0:GW], vv[0][:, t, :], vv[1][:, t, :], tok,
                                    proj_hi_done, proj_lo_done, last_reader)
            proj_free[i] = ready
            v_ready[G, t] = ready
            if t == TT - 1:
                retire(("v", b, g), tok)

        def key_tiles(i):
            return list(range(max(i - 1, 0), min(i + 2, TT)))

        s_free = [None, None]
        prob_free = [None, None]
        normed = {}
        pt_ready = {}
        t_free = [()]

        def scores(H, i):
            s = (H * TT + i) % 2
            js = key_tiles(i)
            n = len(js) * P
            pe.wait(s_free[s], *q_ready[H, i // 4])
            for c in sorted({j // 4 for j in js}):
                pe.wait(*k_ready[H, c])
            rows_, keys = slice(i * P, (i + 1) * P), slice(js[0] * P, js[0] * P + n)
            bankS = sbank[s]
            three_passes(bankS[:, 0:n], [([qT[0][:, rows_], qT[1][:, rows_]],
                                          [kT[0][:, keys], kT[1][:, keys]])], True, False)
            lead, trail = i > 0, i < TT - 1
            if lead and trail:
                dst = strided(bankS[:, 0:BLK], 0, n - BLK, 2, BLK)
                rhs = mask_r[:, :].rearrange("p (a b) -> p a b", a=2)
            elif trail:
                dst, rhs = bankS[:, n - BLK:n], mask_r[:, BLK:P]
            else:
                dst, rhs = bankS[:, 0:BLK], mask_r[:, 0:BLK]
            tok = pe.do(lambda e: e.matmul(dst, mask_l[:], rhs, start=False, stop=True), scored)
            s_done[H, i] = tok

        def softmax(H, i):
            u = H * TT + i
            s, n = u % 2, len(key_tiles(i)) * P
            c = (u % 2) * 4
            mx, nm, sm, rc = (stat[:, c + j:c + j + 1] for j in range(4))
            pr = prob[u % 2]
            dve.wait(s_done[H, i])
            t = dve.do(lambda e: e.reduce_max(mx, sbank[s][:, 0:n], AX), max_done)
            dve.wait(t)
            t = dve.do(lambda e: e.tensor_scalar(nm, mx, -SCALE, None, ALU.mult), negmax_done)
            act.wait(t, prob_free[u % 2])
            t = act.do(lambda e: e.activation(pr[:, 0:n], sbank[s][:, 0:n], ACT.Exp, bias=nm, scale=SCALE,
                                              accum_out=sm), exp_done)
            s_free[s] = t
            normed[H, i] = (t, pr, sm, rc, n)

        def normalise(H, i):
            t, pr, sm, rc, n = normed[H, i]
            dve.wait(t)
            t = dve.do(lambda e: e.reciprocal(rc, sm), recip_done)
            dve.wait(t)
            normed[H, i] = dve.do(lambda e: e.tensor_scalar(pr[:, 0:n], pr[:, 0:n], rc, None, ALU.mult), norm_done)

        def turn_probs(H, i):
            u = H * TT + i
            pr = prob[u % 2]
            js = key_tiles(i)
            pe.wait(normed[H, i], *t_free[0])
            for m, j in enumerate(js):
                tok = pe.do(lambda e, m=m: e.transpose(tbank[:, m * P:(m + 1) * P], pr[:, m * P:(m + 1) * P],
                                                       ident[:]), turned if j == js[-1] else None)
            prob_free[u % 2] = tok
            n = len(js)
            src = tbank[:, 0:n * P].rearrange("p (m q) -> p m q", m=n)
            o = js[0] * 3 * P + (i - js[0] + 1) * P
            dst = [strided(pT[z], o, 2 * P, n, P) for z in range(2)]
            pt_ready[H, i] = split_from_psum(src, dst[0], dst[1], tok, pt_hi_done, pt_lo_done,
                                             *(pv_done.get((H - 1, j)) for j in js))
            t_free[0] = pt_ready[H, i]

        o_free = [(), ()]
        o_ready = {}
        wo_done = {}

        def weigh_values(H, j):
            G, h = H // HG, H % NH
            pe.wait(*v_ready[G, j], *pt_ready[H, min(j + 1, TT - 1)])
            hc = slice((H % HG) * HD, (H % HG + 1) * HD)
            v_ = [vv[z][:, j, hc] for z in range(2)]
            tiles = key_tiles(j)
            for half in (0, 1):
                mine = [i for i in tiles if i // 4 == half]
                if not mine:
                    continue
                first = (half == 0 and j == 0) or (half == 1 and j == 3)
                if first:
                    pe.wait(*o_free[half])
                o = j * 3 * P + (mine[0] - j + 1) * P
                n = len(mine) * P
                c = (mine[0] % 4) * P
                last = (half == 0 and j == 4) or (half == 1 and j == TT - 1)
                tok = three_passes(obank[half][:, c:c + n],
                                   [(v_, [pT[z][:, o:o + n] for z in range(2)])], first, last,
                                   attended, skip=True)
                if last:
                    slot = H % O_SLOTS
                    cols = slice(half * CH, half * CH + CH)
                    o_ready[H, half] = split_from_psum(obank[half][:, :], oT[slot][0][:, cols],
                                                       oT[slot][1][:, cols], tok, o_hi_done, o_lo_done,
                                                       wo_done.get((H - O_SLOTS) // HG))
                    o_free[half] = o_ready[H, half]
            pv_done[H, j] = tok

        y_free = [None]
        y_sum = {}

        def project_out(G, t):
            b, g = divmod(G, NG)
            w = piece(("o", b, g))
            w2 = [half.rearrange("p (k n) -> p k n", k=HG) for half in w]
            for hl in range(HG):
                pe.wait(*o_ready[HG * G + hl, t // 4])
            pe.wait(y_free[0])
            cols = slice(t * P, (t + 1) * P)
            tok = three_passes(ybank[:, :], [([oT[(HG * G + hl) % O_SLOTS][z][:, cols] for z in range(2)],
                                              [w2[z][:, hl, :] for z in range(2)]) for hl in range(HG)],
                               True, True, y_made)
            dve.wait(tok, y_sum[b, t])
            y_sum[b, t] = y_free[0] = dve.do(
                lambda e: e.tensor_tensor(yacc[:, t, :], ybank[:, :], yacc[:, t, :], ALU.add), y_added)
            if t == TT - 1:
                wo_done[G] = tok
                retire(("o", b, g), tok)

        def scratch(name, n=1, dt=F32):
            return sb(name, [P, n], dt)

        bn_out, mv, tmp, rstd = ([scratch(f"{nm}{i}", n) for i in range(2)]
                                 for nm, n in (("bn_out", 6), ("mv", 2), ("tmp", 1), ("rstd", 1)))
        neg_half = scratch("neg_half")
        score = scratch("score", NB * TT)
        ln1, ln2 = scratch("ln1", D), scratch("ln2", D)
        low = scratch("low", P, BF16)
        column = scratch("column", P, BF16)
        upper = scratch("upper", P, BF16)
        causal = scratch("causal", P, BF16)
        ident_bf = scratch("ident_bf", P, BF16)
        ones_bf = scratch("ones_bf", P, BF16)
        products = scratch("products", D, BF16)
        counts = scratch("counts", 3 * TT)
        rank, before = scratch("rank", TT), scratch("before", TT)
        chosen = scratch("chosen", TT, BF16)
        place = work[5][:].bitcast(BF16)
        position, row_index = ([scratch(f"{nm}{b}", 1, I32) for b in range(NB)] for nm in ("position", "row_index"))
        x_sel = [scratch(f"x_sel{b}", D) for b in range(NB)]
        rope_sel = [scratch(f"rope_sel{b}", 2 * HD) for b in range(NB)]
        gate = scratch("gate", 4 * NB)

        small_ready = signal("small_ready")
        bcast_loaded = signal("bcast_loaded")
        for dst, src in ((router, w_router), (ln1, ln1_w), (ln2, ln2_w)):
            bcast = sp.do(lambda e, dst=dst, src=src: e.dma_start(
                dst[:], bass.AP(tensor=src.tensor, offset=src.offset, ap=[[0, P], [1, D]])), bcast_loaded, 16)
        for dst, value in ((low, 1.0), (upper, 1.0), (causal, 0.0), (ident_bf, 0.0)):
            t = pool.do(lambda e, dst=dst, value=value: e.memset(dst[:], value), small_ready)
        pool.wait(t)
        pool.do(lambda e: e.affine_select(out=low[:], in_=low[:], compare_op=ALU.is_gt, fill=0.0, base=0,
                                          pattern=[[-1, P]], channel_multiplier=1), small_ready)
        pool.do(lambda e: e.affine_select(out=upper[:], in_=upper[:], compare_op=ALU.is_ge, fill=0.0, base=0,
                                          pattern=[[1, P]], channel_multiplier=-1), small_ready)
        pool.do(lambda e: e.affine_select(out=causal[:], in_=causal[:], compare_op=ALU.is_ge, fill=NEG, base=0,
                                          pattern=[[-1, P]], channel_multiplier=1), small_ready)
        pool.do(lambda e: e.affine_select(out=ident_bf[:], in_=ident_bf[:], compare_op=ALU.not_equal, fill=1.0,
                                          base=0, pattern=[[-1, P]], channel_multiplier=1), small_ready)
        pool_small = pool.do(lambda e: e.iota(column[:], pattern=[[1, P]], base=0, channel_multiplier=0,
                                              allow_small_or_imprecise_dtypes=True), small_ready)
        dve_small_ready = signal("dve_small_ready")
        dve.do(lambda e: e.memset(neg_half[:], -0.5), dve_small_ready)
        dve.do(lambda e: e.memset(counts[:], 0.0), dve_small_ready)
        dve_small = dve.do(lambda e: e.memset(ones_bf[:], 1.0), dve_small_ready)

        ln_step, rstd_step, layer2_step = signal("ln_step"), signal("rstd_step"), signal("layer2_step")
        act_step, pe_step = signal("act_step"), signal("pe_step")
        y_stored = [signal(f"y_stored{t}") for t in range(TT)]
        out_stored = [signal(f"out_stored{i}") for i in range(2)]

        def dve_then(fn, sig=None):
            t = dve.do(fn, sig or ln_step)
            dve.wait(t)
            return t

        def inverse_root(after, dst, buf, src, mult, eps):
            pool.wait(after, dve_small)
            t = pool.do(lambda e: e.tensor_scalar(buf, src, mult, eps, ALU.mult, ALU.add), rstd_step)
            pool.wait(t)
            return pool.do(lambda e: e.tensor_tensor(dst, buf, neg_half[:], ALU.pow), rstd_step)

        def moments(src, i):
            dve_then(lambda e: e.bn_stats(bn_out[i][:], src))
            return dve_then(lambda e: e.bn_aggr(mv[i][:], bn_out[i][:]))

        scored_tile = {}
        rstd_read = [None, None]

        def finish_layer1(b, t):
            i = t % 2
            row = yacc[:, t, :]
            dve.wait(y_sum[b, t])
            stats = moments(row, i)
            r = inverse_root(stats, rstd[i][:], tmp[i][:], mv[i][:, 1:2], 1.0, LN_EPS)
            yield
            dve.wait(r)
            normal = dve_then(lambda e: e.tensor_scalar(row, row, mv[i][:, 0:1], rstd[i][:], ALU.subtract, ALU.mult))
            sp.wait(normal)
            stored = sp.do(lambda e: e.dma_start(y_dram[b][t * P:(t + 1) * P, :], row), y_stored[t], 16)
            stats = moments(row, i)
            r = inverse_root(stats, rstd[i][:], tmp[i][:], mv[i][:, 1:2], 4.0, LN_EPS)
            dve.wait(bcast)
            scored_tile[b, t] = dve.do(lambda e: e.tensor_tensor_reduce(
                products[:], row, router[:], 1.0, 0.0, ALU.mult, ALU.add, score[:, b * TT + t:b * TT + t + 1]), ln_step)
            yield
            dve.wait(r, scored_tile[b, t])
            dve_then(lambda e: e.tensor_scalar(rstd[i][:], rstd[i][:], 2.0, None, ALU.mult))
            dve.wait(work_free[2 + i])
            t2 = dve.do(lambda e: e.tensor_scalar(work[2 + i][:], row, mv[i][:, 0:1], rstd[i][:], ALU.subtract,
                                                  ALU.mult), ln_step)
            sp.wait(t2)
            work_free[2 + i] = sp.do(lambda e: e.dma_start(out[b, t * P:(t + 1) * P, :], work[2 + i][:]),
                                     out_stored[i], 16)
            if b + 1 < NB:
                sp.wait(stored)
                y_sum[b + 1, t] = load_resid(b + 1, t, t2)

        rows_out = {}
        selected = {}

        def choose(b):
            own = [score[:, b * TT + a:b * TT + a + 1] for a in range(TT)]
            rows_all = [work[3], work[4]]
            row_tok = []
            for half in range(2):
                i = take_proj()
                pe.wait(*[scored_tile[b, a] for a in range(4 * half, 4 * half + 4)])
                for a in range(4):
                    c = own[4 * half + a]
                    wide = bass.AP(tensor=c.tensor, offset=c.offset, ap=[list(c.ap[0]), [0, P]])
                    tok = pe.do(lambda e, i=i, a=a, wide=wide: e.transpose(proj[i][:, a * P:(a + 1) * P], wide, ident[:]),
                                pe_step)
                act.wait(tok, work_free[3 + half])
                t = act.do(lambda e, half=half, i=i: e.activation(rows_all[half][:], proj[i][:, :], ACT.Copy), act_step)
                proj_free[i] = (t,)
                row_tok.append(t)
            yield
            dve.wait(*row_tok, dve_small, pool_small, work_free[2], work_free[5], *(scored_tile[b, a] for a in range(TT)))
            junk = [work[2], work[5]]

            def count(k, a, half, lo, hi, op):
                if lo < hi:
                    dve_then(lambda e: e.tensor_scalar(junk[half][:, lo:hi], rows_all[half][:, lo:hi], own[a], None,
                                                       op, ALU.add, accum_out=counts[:, k * TT + a:k * TT + a + 1]),
                             layer2_step)
            for a in range(TT):
                split = a * P
                for half in range(2):
                    base = half * 512
                    cut = min(max(split - base, 0), 512)
                    if 0 < cut < 512:
                        count(0 if half == 0 else 1, a, half, 0, cut, ALU.is_ge)
                        count(2, a, half, cut, 512, ALU.is_gt)
                    elif cut == 512:
                        count(half, a, half, 0, 512, ALU.is_ge)
                    else:
                        count(half, a, half, 0, 512, ALU.is_gt)
                if a % 4 == 3:
                    yield
            dve_then(lambda e: e.tensor_tensor(rank[:], counts[:, 0:TT], counts[:, TT:2 * TT], ALU.add), layer2_step)
            dve_then(lambda e: e.tensor_tensor(rank[:], rank[:], counts[:, 2 * TT:3 * TT], ALU.add), layer2_step)
            for a in range(TT):
                half, c = divmod(a * P, 512)
                dve_then(lambda e, a=a, half=half, c=c: e.scalar_tensor_tensor(
                    junk[half][:, 0:P], rows_all[half][:, c:c + P], own[a], low[:], ALU.is_equal, ALU.mult,
                    accum_out=counts[:, a:a + 1]), layer2_step)
            t = dve_then(lambda e: e.tensor_tensor(rank[:], rank[:], counts[:, 0:TT], ALU.add), layer2_step)
            work_free[2] = work_free[3] = work_free[4] = work_free[5] = t
            t = dve_then(lambda e: e.tensor_scalar(chosen[:], rank[:], float(KSEL), None, ALU.is_lt), layer2_step)
            i = take_proj()
            pe.wait(t, pool_small, dve_small)
            pe.do(lambda e: e.matmul(proj[i][:, 0:TT], upper[:], chosen[:], start=True, stop=False,
                                     skip_group_check=True))
            for a in range(TT - 1):
                c = chosen[:, a:a + 1]
                wide = bass.AP(tensor=c.tensor, offset=c.offset, ap=[list(c.ap[0]), [0, TT - 1 - a]])
                tok = pe.do(lambda e, a=a, wide=wide: e.matmul(proj[i][:, a + 1:TT], ones_bf[:], wide, start=False,
                                                               stop=a == TT - 2, skip_group_check=True), pe_step)
            yield
            dve.wait(tok)
            t = dve_then(lambda e: e.tensor_copy(before[:], proj[i][:, 0:TT]), layer2_step)
            proj_free[i] = (t,)
            for a in range(TT):
                t = dve_then(lambda e, a=a: e.tensor_scalar(place[:, a * P:(a + 1) * P], column[:], before[:, a:a + 1],
                                                            None, ALU.is_ge), layer2_step)
            j = take_proj()
            pe.wait(t)
            for a in range(TT):
                tok = pe.do(lambda e, a=a: e.matmul(proj[j][:, 0:1], place[:, a * P:(a + 1) * P], ones_bf[:, 0:1],
                                                    start=a == 0, stop=a == TT - 1), pe_step)
            work_free[5] = tok
            yield
            dve.wait(tok)
            dve_then(lambda e: e.tensor_copy(position[b][:], proj[j][:, 0:1]), layer2_step)
            t = dve_then(lambda e: e.tensor_scalar(row_index[b][:], proj[j][:, 0:1], float(b * T), None, ALU.add),
                         layer2_step)
            proj_free[j] = (t,)
            pool.wait(t, *((sig, 16 * (b + 1)) for sig in y_stored))
            sig = gathered[b]
            pool.do(lambda e: e.indirect_dma_start(out=x_sel[b][:], out_offset=None, in_=y_dram[b],
                                                   in_offset=bass.IndirectOffsetOnAxis(ap=position[b][:, 0:1], axis=0)),
                    sig, 16)
            selected[b] = pool.do(lambda e: e.indirect_dma_start(
                out=rope_sel[b][:], out_offset=None, in_=rope[:, :],
                in_offset=bass.IndirectOffsetOnAxis(ap=position[b][:, 0:1], axis=0)), sig, 16)

        gathered = [signal(f"gathered{b}") for b in range(NB)]

        NT = NSEL
        q2T = [carve(start["xT"] + z * XT_N, NH, NT) for z in range(2)]
        k2T = [carve(start["q"] + z * NKV * NT, NKV, NT) for z in range(2)]
        v2 = [carve(start["v"] + z * NB * NKV * HD, NB, NKV * HD) for z in range(2)]
        o2T = [carve(start["pT"] + z * NH * NT, NH, NT) for z in range(2)]
        slot1, slot2 = start["oT"] + 2 * O_N, start["oT"] + 4 * O_N
        hT = [carve(slot2 + z * D, KT, P) for z in range(2)]
        p2T = [carve(slot2 + 2 * D + z * D, D) for z in range(2)]
        h2T = [carve(slot1 + z * KT * NT, KT, NT) for z in range(2)]
        A_SLOTS = 8
        aT = [[carve(start["xT"] + (2 * s + z) * NT, NT) for z in range(2)] for s in range(A_SLOTS)]

        def rms_norm(b, src, weight, dst, free, after, buf):
            dve.wait(after, free)
            t = dve_then(lambda e: e.tensor_tensor_reduce(dst, src, src, 1.0, 0.0, ALU.mult, ALU.add, buf),
                         layer2_step)
            r = inverse_root(t, buf, buf, buf, 1.0 / D, RMS_EPS)
            yield
            dve.wait(r, bcast)
            return_tok[0] = dve_then(lambda e: e.scalar_tensor_tensor(dst, src, buf, weight[:], ALU.mult, ALU.mult),
                                     layer2_step)

        return_tok = [None]

        def transpose_rows(src, ready, dst_hi, dst_lo, *free):
            i = take_proj()
            pe.wait(ready)
            for k in range(KT):
                tok = pe.do(lambda e, k=k: e.transpose(proj[i][:, k * P:(k + 1) * P], src[:, k * P:(k + 1) * P],
                                                       ident[:]), pe_step if k == KT - 1 else None)
            view = proj[i][:, :].rearrange("p (k n) -> p k n", k=KT)
            ready = split_from_psum(view, dst_hi, dst_lo, tok, act_step, layer2_step, *free)
            proj_free[i] = ready
            return tok, ready

        h_ready = {}
        qkv_ready = {}
        bias_loaded = [signal("bias_loaded0"), signal("bias_loaded1")]
        rope_done = signal("rope_done")
        last_qkv = {}

        def routed_in(b):
            dve.wait(selected[b], bcast)
            g = gate[:, 4 * b:4 * b + 4]
            t = dve_then(lambda e: e.tensor_tensor_reduce(products[:], x_sel[b][:], router[:], 1.0, 0.0, ALU.mult,
                                                          ALU.add, g[:, 0:1]), layer2_step)
            act.wait(t)
            t = act.do(lambda e: e.activation(g[:, 1:2], g[:, 0:1], ACT.Exp, scale=-1.0), act_step)
            yield from rms_norm(b, x_sel[b][:], ln1, work[5][:], work_free[5], t, g[:, 3:4])
            ready = return_tok[0]
            dve_then(lambda e: e.tensor_scalar(g[:, 1:2], g[:, 1:2], 1.0, None, ALU.add), layer2_step)
            dve_then(lambda e: e.reciprocal(g[:, 1:2], g[:, 1:2]), layer2_step)
            dve_then(lambda e: e.tensor_scalar(g[:, 2:3], g[:, 1:2], -1.0, 1.0, ALU.mult, ALU.add), layer2_step)
            work_free[5], h_ready[b] = transpose_rows(work[5], ready, hT[0], hT[1], wo_done[NB * NG - 2],
                                                      last_qkv.get(b - 1))

        def project2(b, which, c):
            bias = dict(q=bq, k=bk, v=bv)[which]
            bs = c % 2
            sp.wait(work_free[bs])
            loaded = sp.do(lambda e: e.dma_start(work[bs][:], bass.AP(
                tensor=bias.tensor, offset=bias.offset + c * 512, ap=[[0, P], [1, 512]])), bias_loaded[bs], 16)
            i = take_proj()
            for half in range(2):
                key = (which + "2", b, 2 * c + half)
                w4 = [z.rearrange("p (k n) -> p k n", k=KT) for z in piece(key)]
                pe.wait(*h_ready[b])
                tok = three_passes(proj[i][:, half * GW:(half + 1) * GW],
                                   [([hT[0][:, k, :], hT[1][:, k, :]], [w4[0][:, k, :], w4[1][:, k, :]])
                                    for k in range(KT)], half == 0, half == 1, projected, skip=True)
                retire(key, tok)
            last_qkv[b] = tok
            dve.wait(tok, loaded)
            t = dve_then(lambda e: e.tensor_tensor(work[bs][:], proj[i][:, :], work[bs][:], ALU.add), layer2_step)
            proj_free[i] = (t,)
            if which == "v":
                hi, lo = (v2[z][:, b, c * 512:(c + 1) * 512] for z in range(2))
                act.wait(t, pv_done[NHEADS - 1, TT - 1])
                t_hi = act.do(lambda e: e.activation(hi, work[bs][:], ACT.Copy), act_step)
                dve.wait(t_hi)
                t_lo = dve.do(lambda e: e.tensor_tensor(lo, work[bs][:], hi.bitcast(F32), ALU.subtract), layer2_step)
                work_free[bs] = t_lo
                qkv_ready[which, b, c] = (t_hi, t_lo)
                return
            a, m = 2 + bs, 4 + bs
            cosf = rope_sel[b][:, 0:HD]
            sinf = rope_sel[b][:, HD:2 * HD]

            def over_heads(ap, n):
                return bass.AP(tensor=ap.tensor, offset=ap.offset, ap=[list(ap.ap[0]), [0, 4], [1, n]])

            heads = work[bs][:].rearrange("p (h d) -> p h d", h=4)
            by_cos = work[a][:].rearrange("p (h d) -> p h d", h=4)
            by_sin = work[m][:].rearrange("p (h d) -> p h d", h=4)
            pool.wait(t, work_free[a], selected[b])
            tc = pool.do(lambda e: e.tensor_tensor(by_cos, heads, over_heads(cosf, HD), ALU.mult), rope_done)
            dve.wait(work_free[m], selected[b])
            H2 = HD // 2
            dve.do(lambda e: e.tensor_tensor(by_sin[:, :, 0:H2], heads[:, :, H2:HD], over_heads(sinf[:, 0:H2], H2),
                                             ALU.mult), layer2_step)
            t = dve_then(lambda e: e.tensor_tensor(by_sin[:, :, H2:HD], heads[:, :, 0:H2],
                                                   over_heads(sinf[:, H2:HD], H2), ALU.mult), layer2_step)
            dve.wait(tc)
            t = dve_then(lambda e: e.tensor_tensor(work[m][:], work[a][:], work[m][:], ALU.add), layer2_step)
            work_free[bs] = work_free[a] = t
            yield
            dst = q2T if which == "q" else k2T
            views = [dst[z][:, 4 * c:4 * c + 4, b * P:(b + 1) * P] for z in range(2)]
            work_free[m], qkv_ready[which, b, c] = transpose_rows(
                work[m], t, views[0], views[1], pv_done[NHEADS - 1, TT - 1])

        p2_free = [None]
        prob2_free = [None, None]
        o2_ready = {}

        def attend2(b, n):
            nk = (b + 1) * P
            s = n % 2
            pr = work[s]
            pe.wait(s_free[s], *qkv_ready["q", b, n // 2])
            for bb in range(b + 1):
                pe.wait(*qkv_ready["k", bb, n // 4])
            for h in range(2):
                three_passes(sbank[s][:, h * nk:(h + 1) * nk],
                             [([q2T[z][:, 2 * n + h, b * P:(b + 1) * P] for z in range(2)],
                               [k2T[z][:, n, 0:nk] for z in range(2)])], h == 0, False, skip=True)
                tok = pe.do(lambda e, h=h: e.matmul(sbank[s][:, (h + 1) * nk - P:(h + 1) * nk], ident_bf[:], causal[:],
                                                    start=False, stop=h == 1, skip_group_check=True), scored)
            c = s * 8
            mx, nm, sm, rc = (stat[:, 16 + c + 2 * j:16 + c + 2 * j + 2] for j in range(4))
            dve.wait(tok)
            src = sbank[s][:, 0:2 * nk].rearrange("p (h k) -> p h k", h=2)
            dve_then(lambda e: e.tensor_reduce(mx, src, AX, ALU.max), layer2_step)
            t = dve_then(lambda e: e.tensor_scalar(nm, mx, -SCALE, None, ALU.mult), layer2_step)
            act.wait(t, work_free[s])
            for h in range(2):
                t = act.do(lambda e, h=h: e.activation(pr[:, h * nk:(h + 1) * nk], sbank[s][:, h * nk:(h + 1) * nk],
                                                       ACT.Exp, bias=nm[:, h:h + 1], scale=SCALE,
                                                       accum_out=sm[:, h:h + 1]), exp_done)
            s_free[s] = t
            yield
            dve.wait(t)
            dve_then(lambda e: e.reciprocal(rc, sm), layer2_step)
            wide = bass.AP(tensor=rc.tensor, offset=rc.offset, ap=[list(rc.ap[0]), [1, 2], [0, nk]])
            pv = pr[:, 0:2 * nk].rearrange("p (h k) -> p h k", h=2)
            t = dve_then(lambda e: e.tensor_tensor(pv, pv, wide, ALU.mult), layer2_step)
            pe.wait(t, *t_free[0])
            for kt in range(b + 1):
                for h in range(2):
                    tok = pe.do(lambda e, kt=kt, h=h: e.transpose(
                        tbank[:, (2 * kt + h) * P:(2 * kt + h + 1) * P],
                        pr[:, h * nk + kt * P:h * nk + (kt + 1) * P], ident[:]), pe_step)
            work_free[s] = tok
            w = 2 * P * (b + 1)
            ready = t_free[0] = split_from_psum(tbank[:, 0:w], p2T[0][:, 0:w], p2T[1][:, 0:w], tok, act_step,
                                                layer2_step, p2_free[0])
            yield
            pe.wait(*ready, y_free[0])
            for bb in range(b + 1):
                pe.wait(*qkv_ready["v", bb, n // 4])
            tok = three_passes(ybank[:, 0:2 * P],
                               [([v2[z][:, kt, n * HD:(n + 1) * HD] for z in range(2)],
                                 [p2T[z][:, kt * 2 * P:(kt + 1) * 2 * P] for z in range(2)])
                                for kt in range(b + 1)], True, True, attended)
            p2_free[0] = tok
            src2 = ybank[:, 0:2 * P].rearrange("p (h q) -> p h q", h=2)
            views = [o2T[z][:, 2 * n:2 * n + 2, b * P:(b + 1) * P] for z in range(2)]
            o2_ready[b, n] = split_from_psum(src2, views[0], views[1], tok, act_step, layer2_step,
                                             wo_done[NB * NG - 1])
            y_free[0] = o2_ready[b, n][1]

        def output2(c):
            w2 = [z.rearrange("p (k n) -> p k n", k=HG) for z in piece(("o2", 0, c))]
            for b in range(NB):
                if c == 0:
                    pe.wait(*o_free[b])
                pe.wait(*o2_ready[b, c])
                tok = three_passes(obank[b][:, :], [([o2T[z][:, 2 * c + h, b * P:(b + 1) * P] for z in range(2)],
                                                     [w2[z][:, h, :] for z in range(2)]) for h in range(HG)],
                                   c == 0, c == NH // HG - 1, pe_step)
            retire(("o2", 0, c), tok)
            return tok

        h2_ready = []
        x1_tiles = {}

        def residual2(b, tok):
            dst = yacc[:, b, :]
            x1_tiles[b] = dst
            dve.wait(tok, *((sig, sig.count) for sig in y_stored + out_stored))
            dve_then(lambda e: e.tensor_tensor(dst, obank[b][:, :], x_sel[b][:], ALU.add), layer2_step)
            h = yacc[:, 2 + b, :]
            yield from rms_norm(b, dst, ln2, h, None, None, gate[:, 4 * b + 3:4 * b + 4])
            _, ready = transpose_rows(h, return_tok[0], h2T[0][:, :, b * P:(b + 1) * P],
                                      h2T[1][:, :, b * P:(b + 1) * P], wo_done[NB * NG - 1])
            h2_ready.extend(ready)

        a_ready, a_used = {}, {}

        def gate_up(c):
            wg = [z.rearrange("p (k n) -> p k n", k=KT) for z in piece(("g2", 0, c))]
            wu = [z.rearrange("p (k n) -> p k n", k=KT) for z in piece(("u2", 0, c))]
            pe.wait(*h2_ready)
            for f in range(2):
                ft = 2 * c + f
                i = take_proj()
                fc = slice(f * P, (f + 1) * P)
                for j, w in enumerate((wg, wu)):
                    tok = three_passes(proj[i][:, j * NT:(j + 1) * NT],
                                       [([w[0][:, k, fc], w[1][:, k, fc]], [h2T[0][:, k, :], h2T[1][:, k, :]])
                                        for k in range(KT)], j == 0, j == 1, projected, skip=True)
                wt = work[ft % 4]
                act.wait(tok, work_free[ft % 4])
                t = act.do(lambda e, i=i, wt=wt: e.activation(wt[:, 0:NT], proj[i][:, 0:NT], ACT.Silu), act_step)
                dve.wait(t)
                t = dve.do(lambda e, i=i, wt=wt: e.tensor_tensor(wt[:, NT:2 * NT], wt[:, 0:NT], proj[i][:, NT:2 * NT],
                                                                 ALU.mult), layer2_step)
                proj_free[i] = (t,)
                hi, lo = aT[ft % A_SLOTS]
                act.wait(t, a_used.get(ft - A_SLOTS), *last_attend2)
                t_hi = act.do(lambda e, hi=hi, wt=wt: e.activation(hi, wt[:, NT:2 * NT], ACT.Copy), act_step)
                pool.wait(t_hi, t)
                t_lo = pool.do(lambda e, hi=hi, lo=lo, wt=wt: e.tensor_tensor(lo, wt[:, NT:2 * NT], hi.bitcast(F32),
                                                                              ALU.subtract), w_lo_done)
                work_free[ft % 4] = t_lo
                a_ready[ft] = (t_hi, t_lo)
            retire(("g2", 0, c), tok)
            retire(("u2", 0, c), tok)

        last_attend2 = []

        def down(c):
            w2 = [z.rearrange("p (k n) -> p k n", k=2) for z in piece(("d2", 0, c))]
            for b in range(NB):
                if c == 0:
                    pe.wait(s_free[b])
                for f in range(2):
                    pe.wait(*a_ready[2 * c + f])
                tok = three_passes(sbank[b][:, :], [([aT[(2 * c + f) % A_SLOTS][z][:, b * P:(b + 1) * P] for z in range(2)],
                                                     [w2[z][:, f, :] for z in range(2)]) for f in range(2)],
                                   c == 0, c == FF // GW - 1, pe_step)
            for f in range(2):
                a_used[2 * c + f] = tok
            retire(("d2", 0, c), tok)
            return tok

        scattered = signal("scattered")

        def finish_layer2(b, tok):
            g = gate[:, 4 * b:4 * b + 4]
            pr = x1_tiles[b]
            dve.wait(tok)
            dve_then(lambda e: e.tensor_tensor(pr, sbank[b][:, :], pr, ALU.add), layer2_step)
            dve_then(lambda e: e.tensor_scalar(pr, pr, g[:, 1:2], None, ALU.mult), layer2_step)
            dve_then(lambda e: e.scalar_tensor_tensor(pr, x_sel[b][:], g[:, 2:3], pr, ALU.mult, ALU.add), layer2_step)
            dve_then(lambda e: e.tensor_tensor(pr, pr, x_sel[b][:], ALU.add), layer2_step)
            stats = moments(pr, b)
            r = inverse_root(stats, rstd[b][:], tmp[b][:], mv[b][:, 1:2], 1.0, LN_EPS)
            dve.wait(r)
            t = dve_then(lambda e: e.tensor_scalar(pr, pr, mv[b][:, 0:1], rstd[b][:], ALU.subtract, ALU.mult),
                         layer2_step)
            pool.wait(t, *((sig, sig.count) for sig in out_stored))
            pool.do(lambda e: e.indirect_dma_start(
                out=out.rearrange("b t d -> (b t) d"), in_=pr, in_offset=None,
                out_offset=bass.IndirectOffsetOnAxis(ap=row_index[b][:, 0:1], axis=0)), scattered, 16)

        pump()
        for t in range(TT):
            y_sum[0, t] = load_resid(0, t)
        for t in range(TT):
            turn_x(0, t)
        for which in "kq":
            for c in range(2):
                project_qk(0, which, c)
        for t in range(4):
            project_v(0, t)

        running = []

        def drain(gens):
            for gen in gens:
                for _ in gen:
                    pass

        first2 = [("q", c) for c in range(4)] + [("k", c) for c in range(2)] + [("v", c) for c in range(2)]
        END = NHEADS * TT
        for u in range(END + 16):
            H, i = divmod(u, TT)
            for gen in running:
                next(gen, None)
            live = u < NHEADS * TT
            if live:
                scores(H, i)
                softmax(H, i)
            if u >= 1 and u - 1 < NHEADS * TT:
                turn_probs(*divmod(u - 1, TT))
            if live:
                normalise(H, i)
                if i in (0, 2) and H > 0:
                    project_qk(H, "k" if i == 0 else "q", 1)
                if i in (4, 6) and H + 1 < NHEADS:
                    if i == 4:
                        project_qk(H + 1, "q", 0)
                    else:
                        project_qk(H + 1, "k", 0)
                if H == NH - 1:
                    turn_x(1, i)
            r, G = u % (HG * TT), u // (HG * TT)
            if r >= 12 and G + 1 < NB * NG:
                project_v(G + 1, r - 12)
            if r < 4 and live:
                project_v(G, r + 4)
            if u >= 3 and u - 3 < NHEADS * TT:
                weigh_values(*divmod(u - 3, TT))
            if 4 <= r < 12 and 1 <= G:
                project_out(G - 1, r - 4)
                if (G - 1) % NG == NG - 1:
                    running.append(finish_layer1((G - 1) // NG, r - 4))
            if u in (NG * HG * TT + 15, END + 15):
                running.append(choose(u // END))
            if u == END - 3:
                running.append(routed_in(0))
            if 3 <= u - END < 3 + len(first2):
                running.append(project2(0, *first2[u - END - 3]))

        for c in range(NKV):
            for _ in range(3):
                for gen in running:
                    next(gen, None)
            for _ in attend2(0, c):
                pass
        drain(running)
        drain([routed_in(1)])
        for which, n in (("q", 4), ("k", 2), ("v", 2)):
            for c in range(n):
                drain([project2(1, which, c)])
        for c in range(NKV):
            drain([attend2(1, c)])
            if c >= 1:
                output2(c - 1)
        last_attend2.append(p2_free[0])
        tok = output2(NKV - 1)
        for b in range(NB):
            drain([residual2(b, tok)])
        for c in range(FF // GW):
            gate_up(c)
            if c >= 1:
                down(c - 1)
        tok = down(FF // GW - 1)
        for b in range(NB):
            finish_layer2(b, tok)
        pool.wait((scattered, scattered.count))
        sp.wait(*((sig, sig.count) for sig in y_stored + out_stored))

        block = ctx.enter_context(nc.Block())

        @block.sync
        def _(e):
            sp.replay(e)

        @block.tensor
        def _(e):
            pe.replay(e)

        @block.vector
        def _(e):
            dve.replay(e)

        @block.scalar
        def _(e):
            act.replay(e)

        @block.gpsimd
        def _(e):
            pool.replay(e)


_INS = ["L0_attn_hidden_states", "L0_attn_Wq", "L0_attn_Wk", "L0_attn_Wv", "L0_attn_Wo",
        "L0_ffn_w_router", "L0_ffn_wq", "L0_ffn_bq", "L0_ffn_wk", "L0_ffn_bk", "L0_ffn_wv",
        "L0_ffn_bv", "L0_ffn_wo", "L0_ffn_w_gate", "L0_ffn_w_up", "L0_ffn_w_down",
        "L0_ffn_ln1_w", "L0_ffn_ln2_w"]


def rope_table():
    inv_freq = (1.0 / np.float32(10000.0) ** (np.arange(0, HD, 2, dtype=np.float32) / np.float32(HD)))
    ang = np.arange(T, dtype=np.float32)[:, None] * inv_freq.astype(np.float32)
    c, s = np.cos(ang.astype(np.float64)), np.sin(ang.astype(np.float64))
    return np.concatenate([c, c, -s, s], axis=1).astype(np.float32)


def kernel(**inputs):
    import concourse.bacc as bacc
    from concourse.bass_utils import run_bass_kernel_spmd as run

    nc = bacc.Bacc("TRN2", target_bir_lowering=False, num_devices=1)
    arrays, args = {}, []
    for name in _INS:
        a = np.ascontiguousarray(inputs[name])
        arrays[f"in_{name}"] = a
        args.append(nc.dram_tensor(f"in_{name}", a.shape, mybir.dt.from_np(a.dtype), kind="ExternalInput").ap())
    arrays["rope"] = rope_table()
    args.append(nc.dram_tensor("rope", arrays["rope"].shape, F32, kind="ExternalInput").ap())
    out = nc.dram_tensor("out", (NB, T, D), F32, kind="ExternalOutput").ap()
    build(nc, *args, out)
    r = run(nc, [arrays], core_ids=[0])
    return r.results[0]["out"]
```

```python
from contextlib import ExitStack

import itertools

import numpy as np

import concourse.bass as bass
from concourse import mybir

F32 = mybir.dt.float32
F32R = mybir.dt.float32r
BF16 = mybir.dt.bfloat16
I32 = mybir.dt.int32
ALU = mybir.AluOpType
ACT = mybir.ActivationFunctionType
AX = mybir.AxisListType.X

P = 128
NB, T, D = 2, 1024, 512
KT = D // P
TT = T // P
HD = 128
NH = 16
BLK = 64
HG = 2
NG = NH // HG
GW = HG * HD
PIECE = KT * GW
SCALE = float(HD) ** -0.5
NEG = -1e30
LN_EPS, RMS_EPS = 1e-5, 1e-6
KSEL = T // 8
NKV = 8
FF = 2048
NSEL = NB * KSEL
SPLIT_SLOTS, RAW_SLOTS = 5, 3
O_SLOTS = 3


QKV_ORDER = (("q", 0), ("k", 0), ("q", 1), ("q", 2), ("k", 1), ("q", 3), ("v", 0), ("v", 1))


class Signal:

    def __init__(self, sem):
        self.sem, self.count = sem, 0


class Queue:

    def __init__(self):
        self.items, self.reached = [], {}

    def wait(self, *tokens):
        for token in tokens:
            if token is None:
                continue
            sig, value = token
            if self.reached.get(sig, 0) < value:
                self.reached[sig] = value
                self.items.append(("wait", sig.sem, value))

    def do(self, fn, signal=None, by=1):
        if signal is None:
            self.items.append(("run", fn, None, 0))
            return None
        signal.count += by
        self.items.append(("run", fn, signal.sem, by))
        return signal, signal.count

    def replay(self, eng):
        for item in self.items:
            if item[0] == "wait":
                eng.wait_ge(item[1], item[2])
            else:
                ins = item[1](eng)
                if item[2] is not None:
                    ins.then_inc(item[2], item[3])


def strided(ap, offset, step, count, width):
    return bass.AP(tensor=ap.tensor, offset=ap.offset + offset,
                   ap=[list(ap.ap[0]), [step, count], [1, width]])


def build(nc, x, Wq, Wk, Wv, Wo, w_router, wq, bq, wk, bk, wv, bv, wo, w_gate, w_up, w_down,
          ln1_w, ln2_w, rope, out):
    with ExitStack() as ctx:
        def sb(name, shape, dt=F32):
            return ctx.enter_context(nc.sbuf_tensor(name, shape, dt))

        def bank(name):
            return ctx.enter_context(nc.psum_tensor(name, [P, 512], F32))

        def signal(name):
            return Signal(ctx.enter_context(nc.semaphore(name)))

        y_dram = [nc.dram_tensor(f"y_dram{b}", [T, D], F32, kind="Internal").ap() for b in range(NB)]

        NHEADS = NB * NH

        XT_N, QK_N, V_N, PT_N, O_N = KT * T, T, TT * GW, TT * 3 * P, T
        sizes = dict(xT=2 * XT_N, q=2 * QK_N, k=2 * QK_N, v=2 * V_N, pT=2 * PT_N, oT=2 * O_SLOTS * O_N,
                     w=2 * SPLIT_SLOTS * PIECE)
        start, at = {}, 0
        for name, n in sizes.items():
            start[name] = at
            at += n
        arena = sb("arena", [P, at], F32R)

        def carve(offset, *shape):
            n = int(np.prod(shape))
            view = arena[:, offset:offset + n]
            if len(shape) == 2:
                return view.rearrange("p (a b) -> p a b", a=shape[0])
            if len(shape) == 3:
                return view.rearrange("p (a b c) -> p a b c", a=shape[0], b=shape[1])
            return view

        xT = [carve(start["xT"] + i * XT_N, KT, T) for i in range(2)]
        qT = [carve(start["q"] + i * QK_N, T) for i in range(2)]
        kT = [carve(start["k"] + i * QK_N, T) for i in range(2)]
        vv = [carve(start["v"] + i * V_N, TT, GW) for i in range(2)]
        pT = [carve(start["pT"] + i * PT_N, TT * 3 * P) for i in range(2)]
        oT = [[carve(start["oT"] + (2 * s + i) * O_N, T) for i in range(2)] for s in range(O_SLOTS)]
        wsp = [[carve(start["w"] + (2 * s + i) * PIECE, PIECE) for i in range(2)] for s in range(SPLIT_SLOTS)]
        yacc = sb("yacc", [P, TT, D])
        wraw = [sb(f"wraw{i}", [P, PIECE]) for i in range(RAW_SLOTS)]
        prob = [sb(f"prob{i}", [P, 4 * P]) for i in range(2)]
        work = [sb(f"work{i}", [P, D]) for i in range(6)]
        ident = sb("ident", [P, P])
        mask_l = sb("mask_l", [P, P], BF16)
        mask_r = sb("mask_r", [P, P], BF16)
        stat = sb("stat", [P, 64])
        router = sb("router", [P, D])

        proj = [bank("proj0"), bank("proj1")]
        sbank = [bank("s0"), bank("s1")]
        tbank = bank("tp")
        obank = [bank("o0"), bank("o1")]
        ybank = bank("y")

        pe, dve, act, pool, sp = Queue(), Queue(), Queue(), Queue(), Queue()

        const_ready = signal("const_ready")
        raw_loaded = [signal(f"raw_loaded{i}") for i in range(RAW_SLOTS)]
        w_hi_done, w_lo_done, w_lo_done_dve = signal("w_hi_done"), signal("w_lo_done"), signal("w_lo_done_dve")
        x_loaded = [signal(f"x_loaded{i}") for i in range(6)]
        x_turned, x_hi_done, x_lo_done = signal("x_turned"), signal("x_hi_done"), signal("x_lo_done")
        projected, proj_hi_done, proj_lo_done = (signal("projected"), signal("proj_hi_done"),
                                                 signal("proj_lo_done"))
        scored, max_done, negmax_done, exp_done, recip_done, norm_done = (
            signal("scored"), signal("max_done"), signal("negmax_done"), signal("exp_done"),
            signal("recip_done"), signal("norm_done"))
        turned, pt_hi_done, pt_lo_done = signal("turned"), signal("pt_hi_done"), signal("pt_lo_done")
        attended, o_hi_done, o_lo_done = signal("attended"), signal("o_hi_done"), signal("o_lo_done")
        y_made, y_added = signal("y_made"), signal("y_added")
        resid_loaded = [signal(f"resid_loaded{t}") for t in range(TT)]

        masks_ready = signal("masks_ready")
        t = pool.do(lambda e: e.memset(ident[:], 0.0), const_ready)
        pool.wait(t)
        consts = pool.do(lambda e: e.affine_select(out=ident[:], in_=ident[:], compare_op=ALU.not_equal, fill=1.0,
                                                   base=0, pattern=[[-1, P]], channel_multiplier=1), const_ready)
        dve.do(lambda e: e.memset(mask_l[:], 0.0), masks_ready)
        t = dve.do(lambda e: e.memset(mask_r[:], 0.0), masks_ready)
        dve.wait(t)
        dve.do(lambda e: e.memset(mask_l[0:1, 0:BLK], 1.0), masks_ready)
        dve.do(lambda e: e.memset(mask_l[32:33, BLK:P], 1.0), masks_ready)
        dve.do(lambda e: e.memset(mask_r[32:33, 0:BLK], NEG), masks_ready)
        t = dve.do(lambda e: e.memset(mask_r[0:1, BLK:P], NEG), masks_ready)
        pe.wait(consts, t)

        def three_passes(out_ap, pairs, start, stop, tail_signal=None, skip=False):
            tok = None
            n = len(pairs)
            for i, (l, r) in enumerate(pairs):
                for j, (a, b) in enumerate(((0, 0), (0, 1), (1, 0))):
                    last = i == n - 1 and j == 2
                    tok = pe.do(lambda e, a=l[a], b=r[b], s=start and i == 0 and j == 0, f=stop and last:
                                e.matmul(out_ap, a, b, start=s, stop=f, skip_group_check=skip),
                                tail_signal if last else None)
            return tok

        def split_from_psum(src, hi, lo, ready, hi_sig, lo_sig, *free):
            act.wait(ready, *free)
            t_hi = act.do(lambda e: e.activation(hi, src, ACT.Copy), hi_sig)
            dve.wait(ready, t_hi, *free)
            t_lo = dve.do(lambda e: e.tensor_tensor(lo, src, hi.bitcast(F32), ALU.subtract), lo_sig)
            return t_hi, t_lo

        stream = []

        def columns(w, c):
            return w[:, c * GW:(c + 1) * GW].rearrange("(k p) n -> p k n", p=P)

        def rows(w, c):
            return w[c * GW:(c + 1) * GW, :].rearrange("(k p) n -> p k n", p=P)

        for b in range(NB):
            for g in range(NG):
                stream += [(("q", b, g), columns(Wq, g)), (("v", b, g), columns(Wv, g)),
                           (("k", b, g), columns(Wk, g))]
                G = b * NG + g
                if G >= 1:
                    stream.append((("o", *divmod(G - 1, NG)), rows(Wo, (G - 1) % NG)))
        stream.append((("o", NB - 1, NG - 1), rows(Wo, NG - 1)))
        for b in range(NB):
            for which, c in QKV_ORDER:
                w = dict(q=wq, k=wk, v=wv)[which]
                stream += [((which + "2", b, 2 * c + half), columns(w, 2 * c + half)) for half in range(2)]
        stream += [(("o2", 0, c), rows(wo, c)) for c in range(NH * HD // GW)]
        for c in range(FF // GW):
            stream += [(("g2", 0, c), columns(w_gate, c)), (("u2", 0, c), columns(w_up, c))]
            if c >= 1:
                stream.append((("d2", 0, c - 1), rows(w_down, c - 1)))
        stream.append((("d2", 0, FF // GW - 1), rows(w_down, FF // GW - 1)))
        number = {key: n for n, (key, _) in enumerate(stream)}
        split_tokens, slot_of, raw_free, loaded = {}, {}, {}, {}
        free_slots = [(s, None) for s in range(SPLIT_SLOTS)]
        split_used = {}
        issued = [0, 0]
        lo_queue = [lambda n: pool]

        def load_next():
            while issued[0] < len(stream) and free_slots and (issued[0] < RAW_SLOTS or issued[0] - RAW_SLOTS in raw_free):
                n = issued[0]
                slot_of[n], split_used[n] = free_slots.pop(0)
                _, src = stream[n]
                raw = wraw[n % RAW_SLOTS]
                sp.wait(*raw_free.get(n - RAW_SLOTS, ()))
                dst = raw[:].rearrange("p (k n) -> p k n", k=src.shape[1])
                loaded[n] = sp.do(lambda e, dst=dst, src=src: e.dma_start(dst, src), raw_loaded[n % RAW_SLOTS], 16)
                issued[0] += 1

        def split_next():
            n = issued[1]
            raw, (hi, lo) = wraw[n % RAW_SLOTS], wsp[slot_of[n]]
            act.wait(loaded[n], split_used[n])
            t_hi = act.do(lambda e: e.activation(hi, raw[:], ACT.Copy), w_hi_done)
            eng = lo_queue[0](n)
            eng.wait(loaded[n], split_used[n], t_hi)
            t_lo = eng.do(lambda e: e.tensor_tensor(lo, raw[:], hi.bitcast(F32), ALU.subtract),
                          w_lo_done if eng is pool else w_lo_done_dve)
            split_tokens[n] = (t_hi, t_lo)
            raw_free[n] = (t_hi, t_lo)
            issued[1] += 1
            load_next()

        def split_loaded(upto):
            while issued[1] < min(upto, issued[0]):
                split_next()

        def piece(key):
            n = number[key]
            split_loaded(n + 1)
            pe.wait(*split_tokens[n])
            return wsp[slot_of[n]]

        def retire(key, token):
            free_slots.append((slot_of[number[key]], token))
            load_next()

        proj_free = [(), ()]
        proj_turn = [0]
        HELD = object()

        def take_proj(i=None):
            if i is None:
                i = proj_turn[0] % 2
                if proj_free[i] is HELD:
                    i = 1 - i
                proj_turn[0] = i + 1
            assert proj_free[i] is not HELD
            pe.wait(*proj_free[i])
            return i

        work_free = [None] * 6
        xT_ready = {}
        xT_last_use = {}

        def load_x(b, t, slots):
            slot = t % slots
            sp.wait(work_free[slot])
            return sp.do(lambda e: e.dma_start(work[slot][:], x[b, t * P:(t + 1) * P, :]), x_loaded[slot], 16)

        def turn_x(b, t, bank=1, slots=2, x_in=None):
            slot = t % slots
            x_in = x_in or load_x(b, t, slots)
            i = take_proj(bank)
            pe.wait(x_in)
            for k in range(KT):
                tok = pe.do(lambda e, k=k: e.transpose(proj[i][:, k * P:(k + 1) * P],
                                                       work[slot][:, k * P:(k + 1) * P], ident[:]),
                            x_turned if k == KT - 1 else None)
            work_free[slot] = tok
            src = proj[i][:, :].rearrange("p (k n) -> p k n", k=KT)
            cols = slice(t * P, (t + 1) * P)
            xT_ready[t] = split_from_psum(src, xT[0][:, :, cols], xT[1][:, :, cols], tok,
                                          x_hi_done, x_lo_done, xT_last_use.get(t))
            proj_free[i] = xT_ready[t]

        def load_resid(b, t, free=None):
            sp.wait(free)
            return sp.do(lambda e: e.dma_start(yacc[:, t, :], x[b, t * P:(t + 1) * P, :]), resid_loaded[t], 16)

        CH = 512
        q_ready, k_ready, v_ready = {}, {}, {}
        s_done = {}
        pv_done = {}

        def project_qk(H, which, c):
            b, h = divmod(H, NH)
            w = piece((which, b, h // HG))
            for t in range(c * 4, c * 4 + 4):
                pe.wait(*xT_ready[t])
            i = take_proj(0)
            hcols = slice((h % HG) * HD, (h % HG + 1) * HD)
            w4 = [half.rearrange("p (k n) -> p k n", k=KT) for half in w]
            cols = slice(c * CH, (c + 1) * CH)
            pairs = [([w4[0][:, k, hcols], w4[1][:, k, hcols]], [xT[0][:, k, cols], xT[1][:, k, cols]])
                     for k in range(KT)]
            three_passes(proj[i][:, :], pairs[:KT // 2], True, False)
            yield
            tok = three_passes(proj[i][:, :], pairs[KT // 2:], False, True, projected)
            for t in range(c * 4, c * 4 + 4):
                xT_last_use[t] = tok
            dst = qT if which == "q" else kT
            last_reader = s_done.get((H - 1, {("q", 0): 3, ("q", 1): 7, ("k", 0): 4, ("k", 1): 7}[which, c]))
            ready = split_from_psum(proj[i][:, :], dst[0][:, cols], dst[1][:, cols], tok,
                                    proj_hi_done, proj_lo_done, last_reader)
            proj_free[i] = ready
            (q_ready if which == "q" else k_ready)[H, c] = ready
            if h % HG == HG - 1 and c == 1:
                retire((which, b, h // HG), tok)

        def project_v(G, t):
            b, g = divmod(G, NG)
            w = piece(("v", b, g))
            pe.wait(*xT_ready[t])
            i = take_proj(1)
            w4 = [half.rearrange("p (k n) -> p k n", k=KT) for half in w]
            cols = slice(t * P, (t + 1) * P)
            tok = three_passes(proj[i][:, 0:GW], [([xT[0][:, k, cols], xT[1][:, k, cols]],
                                                   [w4[0][:, k, :], w4[1][:, k, :]]) for k in range(KT)],
                               True, True, projected)
            xT_last_use[t] = tok
            last_reader = pv_done.get((HG * G - 1, t))
            ready = split_from_psum(proj[i][:, 0:GW], vv[0][:, t, :], vv[1][:, t, :], tok,
                                    proj_hi_done, proj_lo_done, last_reader)
            proj_free[i] = ready
            v_ready[G, t] = ready
            if t == TT - 1:
                retire(("v", b, g), tok)

        def key_tiles(i):
            return list(range(max(i - 1, 0), min(i + 2, TT)))

        s_free = [None, None]
        prob_free = [None, None]
        normed = {}
        pt_ready = {}
        t_free = [()]

        def scores(H, i):
            s = (H * TT + i) % 2
            js = key_tiles(i)
            n = len(js) * P
            pe.wait(s_free[s], *q_ready[H, i // 4])
            for c in sorted({j // 4 for j in js}):
                pe.wait(*k_ready[H, c])
            rows_, keys = slice(i * P, (i + 1) * P), slice(js[0] * P, js[0] * P + n)
            bankS = sbank[s]
            three_passes(bankS[:, 0:n], [([qT[0][:, rows_], qT[1][:, rows_]],
                                          [kT[0][:, keys], kT[1][:, keys]])], True, False)
            lead, trail = i > 0, i < TT - 1
            if lead and trail:
                dst = strided(bankS[:, 0:BLK], 0, n - BLK, 2, BLK)
                rhs = mask_r[:, :].rearrange("p (a b) -> p a b", a=2)
            elif trail:
                dst, rhs = bankS[:, n - BLK:n], mask_r[:, BLK:P]
            else:
                dst, rhs = bankS[:, 0:BLK], mask_r[:, 0:BLK]
            tok = pe.do(lambda e: e.matmul(dst, mask_l[:], rhs, start=False, stop=True), scored)
            s_done[H, i] = tok

        def softmax(H, i):
            u = H * TT + i
            s, n = u % 2, len(key_tiles(i)) * P
            c = (u % 2) * 4
            mx, nm, sm, rc = (stat[:, c + j:c + j + 1] for j in range(4))
            pr = prob[u % 2]
            dve.wait(s_done[H, i])
            t = dve.do(lambda e: e.reduce_max(mx, sbank[s][:, 0:n], AX), max_done)
            dve.wait(t)
            t = dve.do(lambda e: e.tensor_scalar(nm, mx, -SCALE, None, ALU.mult), negmax_done)
            act.wait(t, prob_free[u % 2])
            t = act.do(lambda e: e.activation(pr[:, 0:n], sbank[s][:, 0:n], ACT.Exp, bias=nm, scale=SCALE,
                                              accum_out=sm), exp_done)
            s_free[s] = t
            normed[H, i] = (t, pr, sm, rc, n)

        def normalise(H, i):
            t, pr, sm, rc, n = normed[H, i]
            dve.wait(t)
            t = dve.do(lambda e: e.reciprocal(rc, sm), recip_done)
            dve.wait(t)
            normed[H, i] = dve.do(lambda e: e.tensor_scalar(pr[:, 0:n], pr[:, 0:n], rc, None, ALU.mult), norm_done)

        def turn_probs(H, i):
            u = H * TT + i
            pr = prob[u % 2]
            js = key_tiles(i)
            pe.wait(normed[H, i], *t_free[0])
            for m, j in enumerate(js):
                tok = pe.do(lambda e, m=m: e.transpose(tbank[:, m * P:(m + 1) * P], pr[:, m * P:(m + 1) * P],
                                                       ident[:]), turned if j == js[-1] else None)
            prob_free[u % 2] = tok
            n = len(js)
            src = tbank[:, 0:n * P].rearrange("p (m q) -> p m q", m=n)
            o = js[0] * 3 * P + (i - js[0] + 1) * P
            dst = [strided(pT[z], o, 2 * P, n, P) for z in range(2)]
            pt_ready[H, i] = split_from_psum(src, dst[0], dst[1], tok, pt_hi_done, pt_lo_done,
                                             *(pv_done.get((H - 1, j)) for j in js))
            t_free[0] = pt_ready[H, i]

        o_free = [(), ()]
        o_ready = {}
        wo_done = {}

        def weigh_values(H, j):
            G, h = H // HG, H % NH
            pe.wait(*v_ready[G, j], *pt_ready[H, min(j + 1, TT - 1)])
            hc = slice((H % HG) * HD, (H % HG + 1) * HD)
            v_ = [vv[z][:, j, hc] for z in range(2)]
            tiles = key_tiles(j)
            for half in (0, 1):
                mine = [i for i in tiles if i // 4 == half]
                if not mine:
                    continue
                first = (half == 0 and j == 0) or (half == 1 and j == 3)
                if first:
                    pe.wait(*o_free[half])
                o = j * 3 * P + (mine[0] - j + 1) * P
                n = len(mine) * P
                c = (mine[0] % 4) * P
                last = (half == 0 and j == 4) or (half == 1 and j == TT - 1)
                tok = three_passes(obank[half][:, c:c + n],
                                   [(v_, [pT[z][:, o:o + n] for z in range(2)])], first, last,
                                   attended, skip=True)
                if last:
                    slot = H % O_SLOTS
                    cols = slice(half * CH, half * CH + CH)
                    o_ready[H, half] = split_from_psum(obank[half][:, :], oT[slot][0][:, cols],
                                                       oT[slot][1][:, cols], tok, o_hi_done, o_lo_done,
                                                       wo_done.get((H - O_SLOTS) // HG))
                    o_free[half] = o_ready[H, half]
            pv_done[H, j] = tok

        y_free = [None]
        y_sum = {}

        def project_out(G, t):
            b, g = divmod(G, NG)
            w = piece(("o", b, g))
            w2 = [half.rearrange("p (k n) -> p k n", k=HG) for half in w]
            for hl in range(HG):
                pe.wait(*o_ready[HG * G + hl, t // 4])
            last = G == NB * NG - 1
            dst = sbank[t % 2] if last else ybank
            pe.wait(s_free[t % 2] if last else y_free[0])
            cols = slice(t * P, (t + 1) * P)
            tok = three_passes(dst[:, :], [([oT[(HG * G + hl) % O_SLOTS][z][:, cols] for z in range(2)],
                                              [w2[z][:, hl, :] for z in range(2)]) for hl in range(HG)],
                               True, True, y_made)
            dve.wait(tok, y_sum[b, t])
            y_sum[b, t] = dve.do(
                lambda e: e.tensor_tensor(yacc[:, t, :], dst[:, :], yacc[:, t, :], ALU.add), y_added)
            if last:
                s_free[t % 2] = y_sum[b, t]
            else:
                y_free[0] = y_sum[b, t]
            if t == TT - 1:
                wo_done[G] = tok
                retire(("o", b, g), tok)

        def scratch(name, n=1, dt=F32):
            return sb(name, [P, n], dt)

        bn_out, mv, tmp, rstd = ([scratch(f"{nm}{i}", n) for i in range(2)]
                                 for nm, n in (("bn_out", 6), ("mv", 2), ("tmp", 1), ("rstd", 1)))
        neg_half = scratch("neg_half")
        score = scratch("score", NB * TT)
        low = scratch("low", P, BF16)
        column = scratch("column", P, BF16)
        upper = scratch("upper", P, BF16)
        causal = scratch("causal", P, BF16)
        ident_bf = scratch("ident_bf", P, BF16)
        ones_bf = scratch("ones_bf", P, BF16)
        products = scratch("products", D, BF16)
        counts = scratch("counts", 3 * TT)
        rank, before = scratch("rank", TT), scratch("before", TT)
        chosen = scratch("chosen", TT, BF16)
        place = work[5][:].bitcast(BF16)
        position, row_index = ([scratch(f"{nm}{b}", 1, I32) for b in range(NB)] for nm in ("position", "row_index"))
        x_sel = [scratch(f"x_sel{b}", D) for b in range(NB)]
        rope_sel = scratch("rope_sel", 2 * HD)
        gate = scratch("gate", 4 * NB)

        small_ready = signal("small_ready")
        bcast_loaded = signal("bcast_loaded")
        for dst, src in ((router, w_router),):
            bcast = sp.do(lambda e, dst=dst, src=src: e.dma_start(
                dst[:], bass.AP(tensor=src.tensor, offset=src.offset, ap=[[0, P], [1, D]])), bcast_loaded, 16)
        for dst, value in ((low, 1.0), (upper, 1.0), (causal, 0.0), (ident_bf, 0.0)):
            t = pool.do(lambda e, dst=dst, value=value: e.memset(dst[:], value), small_ready)
        pool.wait(t)
        pool.do(lambda e: e.affine_select(out=low[:], in_=low[:], compare_op=ALU.is_gt, fill=0.0, base=0,
                                          pattern=[[-1, P]], channel_multiplier=1), small_ready)
        pool.do(lambda e: e.affine_select(out=upper[:], in_=upper[:], compare_op=ALU.is_ge, fill=0.0, base=0,
                                          pattern=[[1, P]], channel_multiplier=-1), small_ready)
        pool.do(lambda e: e.affine_select(out=causal[:], in_=causal[:], compare_op=ALU.is_ge, fill=NEG, base=0,
                                          pattern=[[-1, P]], channel_multiplier=1), small_ready)
        pool.do(lambda e: e.affine_select(out=ident_bf[:], in_=ident_bf[:], compare_op=ALU.not_equal, fill=1.0,
                                          base=0, pattern=[[-1, P]], channel_multiplier=1), small_ready)
        pool_small = pool.do(lambda e: e.iota(column[:], pattern=[[1, P]], base=0, channel_multiplier=0,
                                              allow_small_or_imprecise_dtypes=True), small_ready)
        dve_small_ready = signal("dve_small_ready")
        dve.do(lambda e: e.memset(neg_half[:], -0.5), dve_small_ready)
        dve.do(lambda e: e.memset(counts[:], 0.0), dve_small_ready)
        dve_small = dve.do(lambda e: e.memset(ones_bf[:], 1.0), dve_small_ready)

        ln_step, rstd_step, layer2_step = signal("ln_step"), signal("rstd_step"), signal("layer2_step")
        act_step, pe_step = signal("act_step"), signal("pe_step")
        y_stored = [signal(f"y_stored{t}") for t in range(TT)]
        out_stored = [signal(f"out_stored{i}") for i in range(2)]

        def dve_then(fn, sig=None):
            t = dve.do(fn, sig or ln_step)
            dve.wait(t)
            return t

        def inverse_root(after, dst, buf, src, mult, eps):
            pool.wait(after, dve_small)
            t = pool.do(lambda e: e.tensor_scalar(buf, src, mult, eps, ALU.mult, ALU.add), rstd_step)
            pool.wait(t)
            return pool.do(lambda e: e.tensor_tensor(dst, buf, neg_half[:], ALU.pow), rstd_step)

        def moments(src, i):
            dve_then(lambda e: e.bn_stats(bn_out[i][:], src))
            return dve_then(lambda e: e.bn_aggr(mv[i][:], bn_out[i][:]))

        scored_tile = {}
        plain = []
        rstd_read = [None, None]

        def finish_layer1(b, t):
            i = t % 2
            row = yacc[:, t, :]
            dve.wait(y_sum[b, t])
            stats = moments(row, i)
            r = inverse_root(stats, rstd[i][:], tmp[i][:], mv[i][:, 1:2], 1.0, LN_EPS)
            yield
            dve.wait(r)
            normal = dve_then(lambda e: e.tensor_scalar(row, row, mv[i][:, 0:1], rstd[i][:], ALU.subtract, ALU.mult))
            sp.wait(normal)
            stored = sp.do(lambda e: e.dma_start(y_dram[b][t * P:(t + 1) * P, :], row), y_stored[t], 16)
            dve.wait(bcast)
            scored_tile[b, t] = dve.do(lambda e: e.tensor_tensor_reduce(
                products[:], row, router[:], 1.0, 0.0, ALU.mult, ALU.add, score[:, b * TT + t:b * TT + t + 1]), ln_step)
            if b + 1 == NB:
                plain.append(finish_plain(b, t, stored))
            else:
                yield
                yield from finish_plain(b, t, stored)

        def finish_plain(b, t, stored):
            i = t % 2
            row = yacc[:, t, :]
            dve.wait(scored_tile[b, t])
            stats = moments(row, i)
            r = inverse_root(stats, rstd[i][:], tmp[i][:], mv[i][:, 1:2], 4.0, LN_EPS)
            yield
            dve.wait(r)
            dve_then(lambda e: e.tensor_scalar(rstd[i][:], rstd[i][:], 2.0, None, ALU.mult))
            dve.wait(work_free[2 + i])
            t2 = dve.do(lambda e: e.tensor_scalar(work[2 + i][:], row, mv[i][:, 0:1], rstd[i][:], ALU.subtract,
                                                  ALU.mult), ln_step)
            sp.wait(t2)
            work_free[2 + i] = sp.do(lambda e: e.dma_start(out[b, t * P:(t + 1) * P, :], work[2 + i][:]),
                                     out_stored[i], 16)
            if b + 1 < NB:
                sp.wait(stored)
                y_sum[b + 1, t] = load_resid(b + 1, t, t2)

        rows_out = {}
        selected = {}

        bank1_free = [True]
        rope_read = []

        def choose(b):
            own = [score[:, b * TT + a:b * TT + a + 1] for a in range(TT)]
            rows_all = [work[3], work[4]]
            row_tok = []
            tail = b == NB - 1

            def take(n):
                if tail:
                    pe.wait(*o_free[n % 2])
                    return obank[n % 2]
                return proj[take_proj(1)]

            def give(n, token):
                if tail:
                    o_free[n % 2] = (token,)
                else:
                    proj_free[1] = (token,)

            for half in range(2):
                while not (tail or bank1_free[0]):
                    yield
                dst = take(half)
                pe.wait(*[scored_tile[b, a] for a in range(4 * half, 4 * half + 4)])
                for a in range(4):
                    c = own[4 * half + a]
                    wide = bass.AP(tensor=c.tensor, offset=c.offset, ap=[list(c.ap[0]), [0, P]])
                    tok = pe.do(lambda e, dst=dst, a=a, wide=wide: e.transpose(dst[:, a * P:(a + 1) * P], wide,
                                                                               ident[:]), pe_step)
                act.wait(tok, work_free[3 + half])
                t = act.do(lambda e, half=half, dst=dst: e.activation(rows_all[half][:], dst[:, :], ACT.Copy), act_step)
                give(half, t)
                row_tok.append(t)
            yield
            dve.wait(*row_tok, dve_small, pool_small, work_free[2], work_free[5], *(scored_tile[b, a] for a in range(TT)))
            junk = [work[2], work[5]]
            turn, turn_tok = [0], [None, None]

            def count(k, a, half, lo, hi, op):
                if lo < hi:
                    turn[0] += 1
                    z = turn[0] % 2
                    dve.wait(turn_tok[z])
                    turn_tok[z] = dve.do(lambda e: e.tensor_scalar(junk[z][:, lo:hi], rows_all[half][:, lo:hi], own[a], None,
                                                       op, ALU.add, accum_out=counts[:, k * TT + a:k * TT + a + 1]),
                             layer2_step)
            for a in range(TT):
                split = a * P
                for half in range(2):
                    base = half * 512
                    cut = min(max(split - base, 0), 512)
                    if 0 < cut < 512:
                        count(0 if half == 0 else 1, a, half, 0, cut, ALU.is_ge)
                        count(2, a, half, cut, 512, ALU.is_gt)
                    elif cut == 512:
                        count(half, a, half, 0, 512, ALU.is_ge)
                    else:
                        count(half, a, half, 0, 512, ALU.is_gt)
                if not tail or a % 4 == 3:
                    yield
            dve.wait((layer2_step, layer2_step.count))
            dve_then(lambda e: e.tensor_tensor(rank[:], counts[:, 0:TT], counts[:, TT:2 * TT], ALU.add), layer2_step)
            dve_then(lambda e: e.tensor_tensor(rank[:], rank[:], counts[:, 2 * TT:3 * TT], ALU.add), layer2_step)
            for a in range(TT):
                half, c = divmod(a * P, 512)
                dve.do(lambda e, a=a, half=half, c=c: e.scalar_tensor_tensor(
                    junk[half][:, c:c + P], rows_all[half][:, c:c + P], own[a], low[:], ALU.is_equal, ALU.mult,
                    accum_out=counts[:, a:a + 1]), layer2_step)
                if not tail and a % 2:
                    yield
            dve.wait((layer2_step, layer2_step.count))
            t = dve_then(lambda e: e.tensor_tensor(rank[:], rank[:], counts[:, 0:TT], ALU.add), layer2_step)
            work_free[2] = work_free[3] = work_free[4] = work_free[5] = t
            t = dve_then(lambda e: e.tensor_scalar(chosen[:], rank[:], float(KSEL), None, ALU.is_lt), layer2_step)
            while not (tail or bank1_free[0]):
                yield
            dst2 = take(0)
            pe.wait(t, pool_small, dve_small)
            pe.do(lambda e: e.matmul(dst2[:, 0:TT], upper[:], chosen[:], start=True, stop=False,
                                     skip_group_check=True))
            for a in range(TT - 1):
                c = chosen[:, a:a + 1]
                wide = bass.AP(tensor=c.tensor, offset=c.offset, ap=[list(c.ap[0]), [0, TT - 1 - a]])
                tok = pe.do(lambda e, a=a, wide=wide: e.matmul(dst2[:, a + 1:TT], ones_bf[:], wide, start=False,
                                                               stop=a == TT - 2, skip_group_check=True), pe_step)
            yield
            dve.wait(tok)
            t = dve_then(lambda e: e.tensor_copy(before[:], dst2[:, 0:TT]), layer2_step)
            give(0, t)
            for a in range(TT):
                t = dve.do(lambda e, a=a: e.tensor_scalar(place[:, a * P:(a + 1) * P], column[:], before[:, a:a + 1],
                                                            None, ALU.is_ge), layer2_step)
            while not (tail or bank1_free[0]):
                yield
            dst3 = take(1)
            pe.wait(t)
            for a in range(TT):
                tok = pe.do(lambda e, a=a: e.matmul(dst3[:, 0:1], place[:, a * P:(a + 1) * P], ones_bf[:, 0:1],
                                                    start=a == 0, stop=a == TT - 1), pe_step)
            work_free[5] = tok
            yield
            dve.wait(tok)
            dve_then(lambda e: e.tensor_copy(position[b][:], dst3[:, 0:1]), layer2_step)
            t = dve_then(lambda e: e.tensor_scalar(row_index[b][:], dst3[:, 0:1], float(b * T), None, ALU.add),
                         layer2_step)
            give(1, t)
            pool.wait(t, *((sig, 16 * (b + 1)) for sig in y_stored))
            sig = gathered[b]
            pool.do(lambda e: e.indirect_dma_start(out=x_sel[b][:], out_offset=None, in_=y_dram[b],
                                                   in_offset=bass.IndirectOffsetOnAxis(ap=position[b][:, 0:1], axis=0)),
                    sig, 16)
            pool.wait(*rope_read)
            selected[b] = pool.do(lambda e: e.indirect_dma_start(
                out=rope_sel[:], out_offset=None, in_=rope[:, :],
                in_offset=bass.IndirectOffsetOnAxis(ap=position[b][:, 0:1], axis=0)), sig, 16)

        gathered = [signal(f"gathered{b}") for b in range(NB)]

        NT = NSEL
        q2T = [carve(start["xT"] + z * XT_N, NH, NT) for z in range(2)]
        k2T = [carve(start["q"] + z * NKV * NT, NKV, NT) for z in range(2)]
        v2 = [carve(start["v"] + z * NB * NKV * HD, NB, NKV * HD) for z in range(2)]
        o2T = [carve(start["pT"] + z * NH * NT, NH, NT) for z in range(2)]
        slot1, slot2 = start["oT"] + 2 * O_N, start["oT"] + 4 * O_N
        hT = [carve(slot2 + z * D, KT, P) for z in range(2)]
        p2T = [carve(slot2 + 2 * D + z * D, D) for z in range(2)]
        h2T = [carve(slot1 + z * KT * NT, KT, NT) for z in range(2)]
        A_SLOTS = 8
        aT = [[carve(start["xT"] + (2 * s + z) * NT, NT) for z in range(2)] for s in range(A_SLOTS)]

        ln_loaded = signal("ln_loaded")
        ln_here = [None]

        def load_ln(slot, src):
            sp.wait(work_free[slot])
            ln_here[0] = sp.do(lambda e: e.dma_start(work[slot][:], bass.AP(
                tensor=src.tensor, offset=src.offset, ap=[[0, P], [1, D]])), ln_loaded, 16)

        def rms_norm(b, src, weight, dst, free, after, buf):
            dve.wait(after, free)
            t = dve_then(lambda e: e.tensor_tensor_reduce(dst, src, src, 1.0, 0.0, ALU.mult, ALU.add, buf),
                         layer2_step)
            r = inverse_root(t, buf, buf, buf, 1.0 / D, RMS_EPS)
            yield
            dve.wait(r, ln_here[0])
            return_tok[0] = dve_then(lambda e: e.scalar_tensor_tensor(dst, src, buf, work[weight][:], ALU.mult,
                                                                      ALU.mult), layer2_step)
            work_free[weight] = return_tok[0]

        return_tok = [None]

        def transpose_rows(src, ready, dst_hi, dst_lo, *free):
            i = take_proj()
            pe.wait(ready)
            for k in range(KT):
                tok = pe.do(lambda e, k=k: e.transpose(proj[i][:, k * P:(k + 1) * P], src[:, k * P:(k + 1) * P],
                                                       ident[:]), pe_step if k == KT - 1 else None)
            view = proj[i][:, :].rearrange("p (k n) -> p k n", k=KT)
            ready = split_from_psum(view, dst_hi, dst_lo, tok, act_step, layer2_step, *free)
            proj_free[i] = ready
            return tok, ready

        h_ready = {}
        qkv_ready = {}
        bias_loaded = [signal("bias_loaded0"), signal("bias_loaded1")]
        rope_done = signal("rope_done")
        last_qkv = {}

        def routed_in(b):
            load_ln(4, ln1_w)
            dve.wait(selected[b], bcast)
            g = gate[:, 4 * b:4 * b + 4]
            t = dve_then(lambda e: e.tensor_tensor_reduce(products[:], x_sel[b][:], router[:], 1.0, 0.0, ALU.mult,
                                                          ALU.add, g[:, 0:1]), layer2_step)
            act.wait(t)
            t = act.do(lambda e: e.activation(g[:, 1:2], g[:, 0:1], ACT.Exp, scale=-1.0), act_step)
            yield from rms_norm(b, x_sel[b][:], 4, work[5][:], work_free[5], t, g[:, 3:4])
            ready = return_tok[0]
            dve_then(lambda e: e.tensor_scalar(g[:, 1:2], g[:, 1:2], 1.0, None, ALU.add), layer2_step)
            dve_then(lambda e: e.reciprocal(g[:, 1:2], g[:, 1:2]), layer2_step)
            dve_then(lambda e: e.tensor_scalar(g[:, 2:3], g[:, 1:2], -1.0, 1.0, ALU.mult, ALU.add), layer2_step)
            work_free[5], h_ready[b] = transpose_rows(work[5], ready, hT[0], hT[1], wo_done[NB * NG - 2],
                                                      last_qkv.get(b - 1))

        def project2(b, n):
            which, c = QKV_ORDER[n]
            bias = dict(q=bq, k=bk, v=bv)[which]
            bs = n % 2
            sp.wait(work_free[bs])
            loaded = sp.do(lambda e: e.dma_start(work[bs][:], bass.AP(
                tensor=bias.tensor, offset=bias.offset + c * 512, ap=[[0, P], [1, 512]])), bias_loaded[bs], 16)
            if b == NB - 1:
                i, banks, free = n % 2, obank, o_free
                pe.wait(*o_free[i])
            elif n % 2:
                i, banks, free = 0, [ybank], y_free
                pe.wait(y_free[0])
            else:
                i, banks, free = take_proj(), proj, proj_free
            dst_bank = banks[i]
            for half in range(2):
                key = (which + "2", b, 2 * c + half)
                w4 = [z.rearrange("p (k n) -> p k n", k=KT) for z in piece(key)]
                pe.wait(*h_ready[b])
                tok = three_passes(dst_bank[:, half * GW:(half + 1) * GW],
                                   [([hT[0][:, k, :], hT[1][:, k, :]], [w4[0][:, k, :], w4[1][:, k, :]])
                                    for k in range(KT)], half == 0, half == 1, projected, skip=True)
                retire(key, tok)
            last_qkv[b] = tok
            if free is proj_free:
                proj_free[i] = HELD
            yield
            dve.wait(tok, loaded)
            t = dve_then(lambda e: e.tensor_tensor(work[bs][:], dst_bank[:, :], work[bs][:], ALU.add), layer2_step)
            free[i] = t if free is y_free else (t,)
            if which == "v":
                hi, lo = (v2[z][:, b, c * 512:(c + 1) * 512] for z in range(2))
                act.wait(t, pv_done[NHEADS - 1, TT - 1])
                t_hi = act.do(lambda e: e.activation(hi, work[bs][:], ACT.Copy), act_step)
                dve.wait(t_hi)
                t_lo = dve.do(lambda e: e.tensor_tensor(lo, work[bs][:], hi.bitcast(F32), ALU.subtract), layer2_step)
                work_free[bs] = t_lo
                qkv_ready[which, b, c] = (t_hi, t_lo)
                return
            a, m = 2 + bs, 4 + bs
            cosf = rope_sel[:, 0:HD]
            sinf = rope_sel[:, HD:2 * HD]

            def over_heads(ap, n):
                return bass.AP(tensor=ap.tensor, offset=ap.offset, ap=[list(ap.ap[0]), [0, 4], [1, n]])

            heads = work[bs][:].rearrange("p (h d) -> p h d", h=4)
            by_cos = work[a][:].rearrange("p (h d) -> p h d", h=4)
            by_sin = work[m][:].rearrange("p (h d) -> p h d", h=4)
            pool.wait(t, work_free[a], selected[b])
            tc = pool.do(lambda e: e.tensor_tensor(by_cos, heads, over_heads(cosf, HD), ALU.mult), rope_done)
            dve.wait(work_free[m], selected[b])
            H2 = HD // 2
            dve.do(lambda e: e.tensor_tensor(by_sin[:, :, 0:H2], heads[:, :, H2:HD], over_heads(sinf[:, 0:H2], H2),
                                             ALU.mult), layer2_step)
            t = dve_then(lambda e: e.tensor_tensor(by_sin[:, :, H2:HD], heads[:, :, 0:H2],
                                                   over_heads(sinf[:, H2:HD], H2), ALU.mult), layer2_step)
            dve.wait(tc)
            t = dve_then(lambda e: e.tensor_tensor(work[m][:], work[a][:], work[m][:], ALU.add), layer2_step)
            work_free[bs] = work_free[a] = t
            rope_read[:] = [t, tc]
            yield
            dst = q2T if which == "q" else k2T
            views = [dst[z][:, 4 * c:4 * c + 4, b * P:(b + 1) * P] for z in range(2)]
            work_free[m], qkv_ready[which, b, c] = transpose_rows(
                work[m], t, views[0], views[1], pv_done[NHEADS - 1, TT - 1])

        p2_free = [None]
        o2_ready = {}

        def attend2(b, n):
            nk = (b + 1) * P
            s = n % 2
            pr = prob[s]
            pe.wait(s_free[s], *qkv_ready["q", b, n // 2])
            for bb in range(b + 1):
                pe.wait(*qkv_ready["k", bb, n // 4])
            for h in range(2):
                three_passes(sbank[s][:, h * nk:(h + 1) * nk],
                             [([q2T[z][:, 2 * n + h, b * P:(b + 1) * P] for z in range(2)],
                               [k2T[z][:, n, 0:nk] for z in range(2)])], h == 0, False, skip=True)
                tok = pe.do(lambda e, h=h: e.matmul(sbank[s][:, (h + 1) * nk - P:(h + 1) * nk], ident_bf[:], causal[:],
                                                    start=False, stop=h == 1, skip_group_check=True), scored)
            c = s * 8
            mx, nm, sm, rc = (stat[:, 16 + c + 2 * j:16 + c + 2 * j + 2] for j in range(4))
            dve.wait(tok)
            src = sbank[s][:, 0:2 * nk].rearrange("p (h k) -> p h k", h=2)
            dve_then(lambda e: e.tensor_reduce(mx, src, AX, ALU.max), layer2_step)
            t = dve_then(lambda e: e.tensor_scalar(nm, mx, -SCALE, None, ALU.mult), layer2_step)
            act.wait(t, prob_free[s])
            for h in range(2):
                t = act.do(lambda e, h=h: e.activation(pr[:, h * nk:(h + 1) * nk], sbank[s][:, h * nk:(h + 1) * nk],
                                                       ACT.Exp, bias=nm[:, h:h + 1], scale=SCALE,
                                                       accum_out=sm[:, h:h + 1]), exp_done)
            s_free[s] = t
            yield
            dve.wait(t)
            dve_then(lambda e: e.reciprocal(rc, sm), layer2_step)
            wide = bass.AP(tensor=rc.tensor, offset=rc.offset, ap=[list(rc.ap[0]), [1, 2], [0, nk]])
            pv = pr[:, 0:2 * nk].rearrange("p (h k) -> p h k", h=2)
            t = dve_then(lambda e: e.tensor_tensor(pv, pv, wide, ALU.mult), layer2_step)
            yield
            pe.wait(t, *t_free[0])
            for kt in range(b + 1):
                for h in range(2):
                    tok = pe.do(lambda e, kt=kt, h=h: e.transpose(
                        tbank[:, (2 * kt + h) * P:(2 * kt + h + 1) * P],
                        pr[:, h * nk + kt * P:h * nk + (kt + 1) * P], ident[:]), pe_step)
            prob_free[s] = tok
            w = 2 * P * (b + 1)
            ready = t_free[0] = split_from_psum(tbank[:, 0:w], p2T[0][:, 0:w], p2T[1][:, 0:w], tok, act_step,
                                                layer2_step, p2_free[0])
            yield
            pe.wait(*ready, y_free[0])
            for bb in range(b + 1):
                pe.wait(*qkv_ready["v", bb, n // 4])
            tok = three_passes(ybank[:, 0:2 * P],
                               [([v2[z][:, kt, n * HD:(n + 1) * HD] for z in range(2)],
                                 [p2T[z][:, kt * 2 * P:(kt + 1) * 2 * P] for z in range(2)])
                                for kt in range(b + 1)], True, True, attended)
            p2_free[0] = tok
            src2 = ybank[:, 0:2 * P].rearrange("p (h q) -> p h q", h=2)
            views = [o2T[z][:, 2 * n:2 * n + 2, b * P:(b + 1) * P] for z in range(2)]
            o2_ready[b, n] = split_from_psum(src2, views[0], views[1], tok, act_step, layer2_step,
                                             wo_done[NB * NG - 1])
            y_free[0] = o2_ready[b, n][1]

        def output2(c):
            w2 = [z.rearrange("p (k n) -> p k n", k=HG) for z in piece(("o2", 0, c))]
            for b in range(NB):
                if c == 0:
                    pe.wait(*o_free[b])
                pe.wait(*o2_ready[b, c])
                tok = three_passes(obank[b][:, :], [([o2T[z][:, 2 * c + h, b * P:(b + 1) * P] for z in range(2)],
                                                     [w2[z][:, h, :] for z in range(2)]) for h in range(HG)],
                                   c == 0, c == NH // HG - 1, pe_step)
            retire(("o2", 0, c), tok)
            return tok

        h2_ready = []
        x1_tiles = {}

        def residual2(b, tok):
            dst = work[4 + b][:]
            x1_tiles[b] = dst
            dve.wait(tok, work_free[4 + b])
            dve_then(lambda e: e.tensor_tensor(dst, obank[b][:, :], x_sel[b][:], ALU.add), layer2_step)
            h = work[b][:]
            yield from rms_norm(b, dst, 2, h, work_free[b], None, gate[:, 4 * b + 3:4 * b + 4])
            work_free[b], ready = transpose_rows(h, return_tok[0], h2T[0][:, :, b * P:(b + 1) * P],
                                      h2T[1][:, :, b * P:(b + 1) * P], wo_done[NB * NG - 1])
            h2_ready.extend(ready)

        a_ready, a_used = {}, {}

        def gate_up(c):
            wg = [z.rearrange("p (k n) -> p k n", k=KT) for z in piece(("g2", 0, c))]
            wu = [z.rearrange("p (k n) -> p k n", k=KT) for z in piece(("u2", 0, c))]
            pe.wait(*h2_ready)
            for f in range(2):
                ft = 2 * c + f
                i = take_proj()
                fc = slice(f * P, (f + 1) * P)
                for j, w in enumerate((wg, wu)):
                    tok = three_passes(proj[i][:, j * NT:(j + 1) * NT],
                                       [([w[0][:, k, fc], w[1][:, k, fc]], [h2T[0][:, k, :], h2T[1][:, k, :]])
                                        for k in range(KT)], j == 0, j == 1, projected, skip=True)
                wt = work[ft % 2]
                act.wait(tok, work_free[ft % 2])
                t = act.do(lambda e, i=i, wt=wt: e.activation(wt[:, 0:NT], proj[i][:, 0:NT], ACT.Silu), act_step)
                dve.wait(t)
                t = dve.do(lambda e, i=i, wt=wt: e.tensor_tensor(wt[:, NT:2 * NT], wt[:, 0:NT], proj[i][:, NT:2 * NT],
                                                                 ALU.mult), layer2_step)
                proj_free[i] = (t,)
                hi, lo = aT[ft % A_SLOTS]
                act.wait(t, a_used.get(ft - A_SLOTS), *last_attend2)
                t_hi = act.do(lambda e, hi=hi, wt=wt: e.activation(hi, wt[:, NT:2 * NT], ACT.Copy), act_step)
                pool.wait(t_hi, t)
                t_lo = pool.do(lambda e, hi=hi, lo=lo, wt=wt: e.tensor_tensor(lo, wt[:, NT:2 * NT], hi.bitcast(F32),
                                                                              ALU.subtract), w_lo_done)
                work_free[ft % 2] = t_lo
                a_ready[ft] = (t_hi, t_lo)
            retire(("g2", 0, c), tok)
            retire(("u2", 0, c), tok)

        last_attend2 = []

        def down(c):
            w2 = [z.rearrange("p (k n) -> p k n", k=2) for z in piece(("d2", 0, c))]
            for b in range(NB):
                if c == 0:
                    pe.wait(s_free[b])
                for f in range(2):
                    pe.wait(*a_ready[2 * c + f])
                tok = three_passes(sbank[b][:, :], [([aT[(2 * c + f) % A_SLOTS][z][:, b * P:(b + 1) * P] for z in range(2)],
                                                     [w2[z][:, f, :] for z in range(2)]) for f in range(2)],
                                   c == 0, c == FF // GW - 1, pe_step)
            for f in range(2):
                a_used[2 * c + f] = tok
            retire(("d2", 0, c), tok)
            return tok

        scattered = signal("scattered")

        def finish_layer2(b, tok):
            g = gate[:, 4 * b:4 * b + 4]
            pr = x1_tiles[b]
            dve.wait(tok)
            dve_then(lambda e: e.tensor_tensor(pr, sbank[b][:, :], pr, ALU.add), layer2_step)
            dve_then(lambda e: e.tensor_scalar(pr, pr, g[:, 1:2], None, ALU.mult), layer2_step)
            dve_then(lambda e: e.scalar_tensor_tensor(pr, x_sel[b][:], g[:, 2:3], pr, ALU.mult, ALU.add), layer2_step)
            dve_then(lambda e: e.tensor_tensor(pr, pr, x_sel[b][:], ALU.add), layer2_step)
            stats = moments(pr, b)
            r = inverse_root(stats, rstd[b][:], tmp[b][:], mv[b][:, 1:2], 1.0, LN_EPS)
            dve.wait(r)
            t = dve_then(lambda e: e.tensor_scalar(pr, pr, mv[b][:, 0:1], rstd[b][:], ALU.subtract, ALU.mult),
                         layer2_step)
            pool.wait(t, *((sig, sig.count) for sig in out_stored))
            pool.do(lambda e: e.indirect_dma_start(
                out=out.rearrange("b t d -> (b t) d"), in_=pr, in_offset=None,
                out_offset=bass.IndirectOffsetOnAxis(ap=row_index[b][:, 0:1], axis=0)), scattered, 16)

        running = []

        def tick():
            for gen in list(running):
                if next(gen, running) is running:
                    running.remove(gen)

        def drain(*gens):
            for gen in gens:
                for _ in gen:
                    pass

        lo_queue[0] = lambda n: dve if n % 2 else pool
        x_in = [load_x(0, t, 6) for t in range(4)]
        load_next()
        x_in += [load_x(0, t, 6) for t in range(4, 6)]
        for t in range(TT):
            turn_x(0, t, t % 2, 6, x_in[t] if t < 6 else None)
            if t == 3:
                drain(project_qk(0, "q", 0))
        for t in range(TT):
            y_sum[0, t] = load_resid(0, t)
        for which, c in (("k", 0), ("q", 1), ("k", 1)):
            drain(project_qk(0, which, c))
        for t in range(4):
            project_v(0, t)
        lo_queue[0] = lambda n: pool

        END = NHEADS * TT
        NORM_STEPS = [4 + 2 * t for t in range(TT)]
        FIRST_STEPS = (1, 2, 3, 4, 6, 7)
        LAST_STEPS = 10
        qk_gen = None
        x_in = []
        for u in range(END + LAST_STEPS):
            H, i = divmod(u, TT)
            r, G = u % (HG * TT), u // (HG * TT)
            was_loaded = issued[0]
            bank1_free[0] = 4 <= r < 11 and G not in (NG - 1,)
            if u < END:
                scores(H, i)
                softmax(H, i)
                if i == 0 and H > 0:
                    qk_gen = project_qk(H, "k", 1)
                if i == 2 and H > 0:
                    qk_gen = project_qk(H, "q", 1)
                if i == 4 and H + 1 < NHEADS:
                    qk_gen = project_qk(H + 1, "q", 0)
                if i == 6 and H + 1 < NHEADS:
                    qk_gen = project_qk(H + 1, "k", 0)
                if qk_gen:
                    next(qk_gen, None)
                if H == NH - 2 and i >= 2:
                    x_in.append(load_x(1, i - 2, 6))
            tick()
            if r >= 12 and G + 1 < NB * NG:
                project_v(G + 1, r - 12)
            if r < 4 and u < END:
                project_v(G, r + 4)
            if 1 <= u <= END:
                turn_probs(*divmod(u - 1, TT))
            if u < END:
                normalise(H, i)
            if u >= 3 and u - 3 < END:
                weigh_values(*divmod(u - 3, TT))
            if H == NH - 1:
                turn_x(1, i, 1, 6, x_in[i])
                if i < TT - 6:
                    x_in.append(load_x(1, i + 6, 6))
            if 4 <= r < 12 and 1 <= G and u < END:
                project_out(G - 1, r - 4)
            if 0 <= u - END < TT:
                project_out(NB * NG - 1, u - END)
                running.append(finish_layer1(NB - 1, u - END))
            if u - 16 * NG in NORM_STEPS:
                running.append(finish_layer1(0, NORM_STEPS.index(u - 16 * NG)))
            if u == NG * HG * TT + 23:
                running.append(choose(0))
            if u == END - 3:
                running.append(routed_in(0))
            if u == END:
                lo_queue[0] = lambda n: dve if n % 3 == 0 else pool
            if u - END in FIRST_STEPS:
                running.append(project2(0, FIRST_STEPS.index(u - END)))
            split_loaded(was_loaded)

        lo_queue[0] = lambda n: dve if n % 2 else pool

        def step(*gens):
            was_loaded = issued[0]
            tick()
            for gen in gens:
                if next(gen, running) is not running:
                    running.append(gen)
            split_loaded(was_loaded)

        running.append(choose(1))
        pairs = iter(range(NKV))
        for n in range(len(FIRST_STEPS), len(QKV_ORDER)):
            step(project2(0, n))
        while len(selected) < NB:
            step(attend2(0, next(pairs)))
        step(routed_in(1), attend2(0, next(pairs)))
        step(attend2(0, next(pairs)))
        while NB - 1 not in h_ready:
            step()
        for k in range(17):
            new = []
            for n in itertools.islice(pairs, 1):
                new.append(attend2(0, n))
            if k < 8:
                new.append(project2(1, k))
            if 5 <= k < 13:
                new.append(attend2(1, k - 5))
            if k >= 9 and k - 9 <= 3:
                tok = output2(k - 9)
            step(*new)
            if k == 11:
                load_ln(2, ln2_w)
            if k >= 13:
                tok = output2(k - 9)
        last_attend2.append(p2_free[0])
        rest = [residual2(b, tok) for b in range(NB)]
        step(*rest)
        step()
        for c in range(FF // GW):
            gate_up(c)
            if c >= 1:
                down(c - 1)
            step(plain[c])
        tok = down(FF // GW - 1)
        while running:
            step()
        for b in range(NB):
            finish_layer2(b, tok)
        pool.wait((scattered, scattered.count))
        sp.wait(*((sig, sig.count) for sig in y_stored + out_stored))

        block = ctx.enter_context(nc.Block())

        @block.sync
        def _(e):
            sp.replay(e)

        @block.tensor
        def _(e):
            pe.replay(e)

        @block.vector
        def _(e):
            dve.replay(e)

        @block.scalar
        def _(e):
            act.replay(e)

        @block.gpsimd
        def _(e):
            pool.replay(e)


_INS = ["L0_attn_hidden_states", "L0_attn_Wq", "L0_attn_Wk", "L0_attn_Wv", "L0_attn_Wo",
        "L0_ffn_w_router", "L0_ffn_wq", "L0_ffn_bq", "L0_ffn_wk", "L0_ffn_bk", "L0_ffn_wv",
        "L0_ffn_bv", "L0_ffn_wo", "L0_ffn_w_gate", "L0_ffn_w_up", "L0_ffn_w_down",
        "L0_ffn_ln1_w", "L0_ffn_ln2_w"]


def rope_table():
    inv_freq = (1.0 / np.float32(10000.0) ** (np.arange(0, HD, 2, dtype=np.float32) / np.float32(HD)))
    ang = np.arange(T, dtype=np.float32)[:, None] * inv_freq.astype(np.float32)
    c, s = np.cos(ang.astype(np.float64)), np.sin(ang.astype(np.float64))
    return np.concatenate([c, c, -s, s], axis=1).astype(np.float32)


def kernel(**inputs):
    import concourse.bacc as bacc
    from concourse.bass_utils import run_bass_kernel_spmd as run

    nc = bacc.Bacc("TRN2", target_bir_lowering=False, num_devices=1)
    arrays, args = {}, []
    for name in _INS:
        a = np.ascontiguousarray(inputs[name])
        arrays[f"in_{name}"] = a
        args.append(nc.dram_tensor(f"in_{name}", a.shape, mybir.dt.from_np(a.dtype), kind="ExternalInput").ap())
    arrays["rope"] = rope_table()
    args.append(nc.dram_tensor("rope", arrays["rope"].shape, F32, kind="ExternalInput").ap())
    out = nc.dram_tensor("out", (NB, T, D), F32, kind="ExternalOutput").ap()
    build(nc, *args, out)
    r = run(nc, [arrays], core_ids=[0])
    return r.results[0]["out"]
```
